# Optimizing a Trainium2 kernel written in Bass

```python
import numpy as np
import jax
import jax.numpy as jnp

def _softmax(x, axis=-1):
    return jax.nn.softmax(x, axis=axis)

def _gelu(x):
    return jax.nn.gelu(x, approximate=True)

def _silu(x):
    return jax.nn.silu(x)

def _sigmoid(x):
    return jax.nn.sigmoid(x)

def _layernorm(x, axis=-1, eps=1e-05):
    m = jnp.mean(x, axis=axis, keepdims=True)
    v = jnp.var(x, axis=axis, keepdims=True)
    return (x - m) / jnp.sqrt(v + eps)

def _scatter_add(tgt, idx, src, axis=0):
    return tgt.at[idx].add(src)

def _segment_sum(src, seg, n):
    return jax.ops.segment_sum(src, seg, n)
kernel_name = 'mk_xattn_seq_d1_seqx_r2_e61799'

def setup_inputs(seed: int=0):
    np.random.seed(seed)
    _w = jnp.asarray

    def _rec_inputs():
        import jax
        import jax.numpy as jnp
        _rk = jax.random.key(seed)
        x = -0.0003482 + 1 * jax.random.normal(jax.random.fold_in(_rk, 1), (2, 2048, 576), jnp.float32)
        _lenS = 2048 - jax.random.randint(jax.random.fold_in(_rk, 7), (2,), 0, max(1, 2048 // 4) + 1, jnp.int32)
        _lenS2 = 128 - jax.random.randint(jax.random.fold_in(_rk, 8), (2,), 0, max(1, 128 // 4) + 1, jnp.int32)
        _ctx_1152P = jax.random.normal(jax.random.fold_in(_rk, 11), (2, 16, 576), jnp.float32)
        _ctx_1152c = jax.random.dirichlet(jax.random.fold_in(_rk, 511), 0.3 * jnp.ones((16,), jnp.float32), (2, 128))
        _ctx_1152t = jnp.einsum('bsk,bkd->bsd', _ctx_1152c, _ctx_1152P)
        _ctx_1152t = _ctx_1152t * jax.lax.rsqrt(jnp.mean(jnp.square(_ctx_1152t)) + 1e-12) * 0.953939
        ctx_1152 = -0.000348611 + 1.00001 * (_ctx_1152t + 0.3 * jax.random.normal(jax.random.fold_in(_rk, 611), (2, 128, 576), jnp.float32))
        return (x, ctx_1152)
    x, ctx_1152 = _rec_inputs()

    def _L0_xattn_setup():
        import jax, jax.numpy as jnp
        import numpy as np
        HEADS = 16
        NUM_VIP = 136
        VIP_SCALE = 1.0

        def _heads(x, h):
            b, s, d = x.shape
            return x.reshape(b, s, h, d // h).transpose(0, 2, 1, 3)

        def _sdpa(q, k, v):
            scale = 1.0 / jnp.sqrt(jnp.asarray(q.shape[-1], q.dtype))
            scores = jnp.einsum('bhqd,bhkd->bhqk', q, k) * scale
            attn = jax.nn.softmax(scores, axis=-1)
            return jnp.einsum('bhqk,bhkd->bhqd', attn, v)
        key = jax.random.key(seed)
        ks = jax.random.split(key, 9)
        d = 576
        w = 0.02
        return {'hidden_states': jax.random.normal(ks[0], (2, 4096, d), jnp.float32), 'encoder_hidden_states': jax.random.normal(ks[1], (2, 286, d), jnp.float32), 'Wq': jax.random.normal(ks[2], (d, d), jnp.float32) * w, 'Wk': jax.random.normal(ks[3], (d, d), jnp.float32) * w, 'Wv': jax.random.normal(ks[4], (d, d), jnp.float32) * w, 'Wo': jax.random.normal(ks[5], (d, d), jnp.float32) * w, 'Wk_vip': jax.random.normal(ks[6], (d, d), jnp.float32) * w, 'Wv_vip': jax.random.normal(ks[7], (d, d), jnp.float32) * w, 'Wo_vip': jax.random.normal(ks[8], (d, d), jnp.float32) * w}
    _L0_xattn_all = _L0_xattn_setup()
    _L0_xattn_in = {k: v for k, v in _L0_xattn_all.items() if k in ('Wq', 'Wk', 'Wv', 'Wo', 'Wk_vip', 'Wv_vip', 'Wo_vip')}
    del _L0_xattn_all
    return {'x': x, 'ctx_1152': ctx_1152, 'L0_xattn_Wq': _L0_xattn_in['Wq'], 'L0_xattn_Wk': _L0_xattn_in['Wk'], 'L0_xattn_Wv': _L0_xattn_in['Wv'], 'L0_xattn_Wo': _L0_xattn_in['Wo'], 'L0_xattn_Wk_vip': _L0_xattn_in['Wk_vip'], 'L0_xattn_Wv_vip': _L0_xattn_in['Wv_vip'], 'L0_xattn_Wo_vip': _L0_xattn_in['Wo_vip']}

def reference(x, ctx_1152, L0_xattn_Wq, L0_xattn_Wk, L0_xattn_Wv, L0_xattn_Wo, L0_xattn_Wk_vip, L0_xattn_Wv_vip, L0_xattn_Wo_vip):
    import jax
    import jax.numpy as jnp

    def _L0_xattn_ref(hidden_states, encoder_hidden_states, Wq, Wk, Wv, Wo, Wk_vip, Wv_vip, Wo_vip):
        import jax, jax.numpy as jnp
        import numpy as np
        HEADS = 16
        NUM_VIP = 136
        VIP_SCALE = 1.0

        def _heads(x, h):
            b, s, d = x.shape
            return x.reshape(b, s, h, d // h).transpose(0, 2, 1, 3)

        def _sdpa(q, k, v):
            scale = 1.0 / jnp.sqrt(jnp.asarray(q.shape[-1], q.dtype))
            scores = jnp.einsum('bhqd,bhkd->bhqk', q, k) * scale
            attn = jax.nn.softmax(scores, axis=-1)
            return jnp.einsum('bhqk,bhkd->bhqd', attn, v)
        residual = hidden_states
        b, sq, d = hidden_states.shape
        seq = encoder_hidden_states.shape[1]
        end_pos = seq - NUM_VIP
        enc = encoder_hidden_states[:, :end_pos, :]
        vip = encoder_hidden_states[:, end_pos:, :]
        lin = lambda x, W: jnp.einsum('bsd,ed->bse', x, W)
        q = _heads(lin(hidden_states, Wq), HEADS)
        k = _heads(lin(enc, Wk), HEADS)
        v = _heads(lin(enc, Wv), HEADS)
        kv = _heads(lin(vip, Wk_vip), HEADS)
        vv = _heads(lin(vip, Wv_vip), HEADS)
        out = _sdpa(q, k, v).transpose(0, 2, 1, 3).reshape(b, sq, d)
        vip_out = _sdpa(q, kv, vv).transpose(0, 2, 1, 3).reshape(b, sq, d)
        out = lin(out, Wo)
        vip_out = lin(vip_out, Wo_vip)
        return out + VIP_SCALE * vip_out + residual
    x = _L0_xattn_ref(x, ctx_1152, L0_xattn_Wq, L0_xattn_Wk, L0_xattn_Wv, L0_xattn_Wo, L0_xattn_Wk_vip, L0_xattn_Wv_vip, L0_xattn_Wo_vip)
    return x

_drawn_inputs = setup_inputs


def setup_inputs(seed=0):
    import zlib

    import numpy as np

    out = dict(_drawn_inputs(seed))
    spreads = {}
    factors = {'L0_xattn_Wq': 3.091, 'L0_xattn_Wk': 5.936, 'L0_xattn_Wk_vip': 3.674}
    for name, (base, spread) in spreads.items():
        noise = np.random.default_rng([zlib.crc32(name.encode()), seed]).standard_normal(out[name].shape)
        drawn = base * np.exp(spread * noise) if base else spread * noise
        out[name] = jnp.asarray(drawn.astype(out[name].dtype))
    for name, factor in factors.items():
        out[name] = (out[name] * factor).astype(out[name].dtype)
    return out
```

```python
from contextlib import ExitStack

import numpy as np

import concourse.bass as bass
from concourse import mybir

F32 = mybir.dt.float32
F32R = mybir.dt.float32r
ALU = mybir.AluOpType
ACT = mybir.ActivationFunctionType
AX = mybir.AxisListType

NUM_VIP = 136
HEADS = 16
P = 128
TOK = 256
BLK = TOK // P
BATCHES = 2
PARTS = 3
CHUNKS = 5
SHARED = 4
VCOLS = 64


def channel_order(head_dim):
    order, sizes = [], []
    for c in range(CHUNKS):
        rows = [head_dim * (PARTS * c + a) + d for a in range(PARTS) for d in range(head_dim)]
        if c < SHARED:
            rows += [head_dim * (HEADS - 1) + SHARED * r + c for r in range(head_dim // SHARED)]
        order += rows
        sizes.append(len(rows))
    return order, sizes


def output_order(head_dim):
    main = [head_dim * h + d for h in range(HEADS) for d in range(32)]
    return main + [head_dim * h + d for h in range(HEADS) for d in range(32, head_dim)]


def build(nc, dram, out):
    D = dram["wq"].shape[0]
    S = dram["x"].shape[1]
    HD = D // HEADS
    KEYS = dram["ctx"].shape[1] // BATCHES
    ENC = (KEYS - NUM_VIP) % KEYS
    VIP = KEYS - ENC
    STEPS = S // TOK
    FULL = D // P
    REST = D - FULL * P
    KC = FULL + 1
    HALF = D // 2
    SCALE = float(HD) ** -0.5
    _, SIZES = channel_order(HD)
    STARTS = [sum(SIZES[:c]) for c in range(CHUNKS)]
    WIDE = max(SIZES)
    LASTR = HD // SHARED
    QROWS = 3 * HD + 4
    MAXROW = 3 * HD
    TAIL = HD - 32
    ONB = HEADS * 32
    VIPCOL = ONB + 2 * HEADS * TAIL
    ONW = VIPCOL + HEADS * VIP
    PAIRS = HEADS // 2
    RING = 3
    assert REST == 64 == HEADS * TAIL and ONW == 6 * P and KEYS == P and HEADS * VIP == P
    assert HD + VIP + 2 <= VCOLS and QROWS <= P and sum(SIZES) == D

    def words(ap):
        return ap.bitcast(F32)

    with ExitStack() as ctx:
        def sem(name):
            return ctx.enter_context(nc.semaphore(name))

        def sb(name, shape, dt=F32, stack=ctx):
            return stack.enter_context(nc.sbuf_tensor(name, shape, dt))

        wq_hi = sb("wq_hi", [P, KC, D], F32R)
        wq_lo = sb("wq_lo", [P, KC, D], F32R)
        wo_hi = sb("wo_hi", [P, KC, D], F32R)
        wo_lo = sb("wo_lo", [P, KC, D], F32R)
        vw_hi = sb("vw_hi", [P, BATCHES, D], F32R)
        vw_lo = sb("vw_lo", [P, BATCHES, D], F32R)
        k_diag = sb("k_diag", [WIDE, BATCHES, CHUNKS, PARTS, KEYS], F32R)
        k_pack = sb("k_pack", [QROWS, BATCHES, HEADS, KEYS], F32R)
        v_ext = sb("v_ext", [KEYS, BATCHES, HEADS, VCOLS])
        ident = sb("ident", [P, P])

        ld_ctx, ld_wk, ld_wkv, ld_wv, ld_wvv, ld_wov, ld_wo, ld_wq, ld_small, ld_vx = (
            sem(n) for n in ("ld_ctx", "ld_wk", "ld_wkv", "ld_wv", "ld_wvv", "ld_wov", "ld_wo", "ld_wq",
                             "ld_small", "ld_vx"))
        kraw_zero, vext_zero, k_ps, kraw_enc, kraw_vip, khi_rdy, klo_rdy, krows_rdy, kpacked = (
            sem(n) for n in ("kraw_zero", "vext_zero", "k_ps", "kraw_enc", "kraw_vip", "khi_rdy",
                             "klo_rdy", "krows_rdy", "kpacked"))
        v_ps, v_rdy, vv_ps, vv_rdy, diag_rdy, vw_ps, vwhi_rdy, vwlo_rdy, wqhi_rdy, wohi_rdy = (
            sem(n) for n in ("v_ps", "v_rdy", "vv_ps", "vv_rdy", "diag_rdy", "vw_ps", "vwhi_rdy",
                             "vwlo_rdy", "wqhi_rdy", "wohi_rdy"))

        with ExitStack() as tmp:
            def st(name, shape, dt=F32):
                return sb(name, shape, dt, tmp)

            raw = {n: st(f"{n}_raw", [P, KC, D]) for n in ("wk", "wkv", "wv", "wvv", "wov", "wo", "wq")}
            ctx_t = st("ctx_t", [P, KC, BATCHES, KEYS])
            k_raw = st("k_raw", [WIDE, CHUNKS, BATCHES, KEYS])
            k_hi = st("k_hi", [WIDE, CHUNKS, BATCHES, KEYS], F32R)
            k_lo = st("k_lo", [WIDE, CHUNKS, BATCHES, KEYS], F32R)
            vv_t = st("vv_t", [P, KC, BATCHES, VIP])
            vv_diag = st("vv_diag", [P, BATCHES, KC, HEADS, VIP])
            mask_part = st("mask_part", [P, PARTS])
            mask_head = st("mask_head", [P, KC, HEADS])
            marks_raw = st("marks_raw", [4, KEYS])
            marks = st("marks", [4, HEADS, KEYS], F32R)

            with ExitStack() as pst:
                def ps(name, shape):
                    return pst.enter_context(nc.psum_tensor(name, shape, F32))

                ps_a = [ps(f"ps_a{i}", [P, 512]) for i in range(2)]
                ps_b = [ps(f"ps_b{i}", [P, 512]) for i in range(2)]
                ps_v = ps("ps_v", [P, 512])
                ps_w = [ps(f"ps_w{i}", [P, 512]) for i in range(2)]
                block = pst.enter_context(nc.Block())

                def rows(name):
                    return dram[name]

                def load(eng, name, landed, twice=False):
                    w = rows(name)
                    dst = raw[name] if name in raw else ctx_t[:].rearrange("p c b k -> p c (b k)")
                    eng.dma_start(dst[:, 0:FULL, :], w[0:FULL * P, :].rearrange("(c p) n -> p c n", p=P)).then_inc(landed, 16)
                    eng.dma_start(dst[0:REST, FULL, :], w[FULL * P:D, :]).then_inc(landed, 16)
                    if twice:
                        eng.dma_start(dst[REST:P, FULL, :], w[FULL * P:D, :]).then_inc(landed, 16)

                def size(kk):
                    return P if kk < FULL else REST

                @block.sync
                def _(sp):
                    load(sp, "ctx", ld_ctx)
                    load(sp, "wk", ld_wk)
                    load(sp, "wkv", ld_wkv)
                    sp.dma_start(mask_part[:], dram["mask_part"]).then_inc(ld_small, 16)
                    sp.dma_start(mask_head[:], dram["mask_head"]).then_inc(ld_small, 16)
                    sp.dma_start(marks_raw[:], dram["marks"]).then_inc(ld_small, 16)
                    sp.dma_start(ident[:], dram["ident"]).then_inc(ld_small, 16)
                    load(sp, "wv", ld_wv)
                    load(sp, "wvv", ld_wvv)
                    load(sp, "wov", ld_wov)
                    load(sp, "wo", ld_wo, twice=True)
                    load(sp, "wq", ld_wq, twice=True)
                    sp.wait_ge(vext_zero, 1)
                    for b in range(BATCHES):
                        sp.dma_start(v_ext[:, b, :, HD:VCOLS], dram["v_const"]).then_inc(ld_vx, 16)
                    sp.wait_ge(khi_rdy, 1)
                    sp.wait_ge(klo_rdy, 1)
                    sp.wait_ge(krows_rdy, 1)
                    for b in range(BATCHES):
                        for row, src in ((0, k_hi), (HD, k_hi), (2 * HD, k_lo)):
                            for a in range(PARTS):
                                sp.dma_start(words(k_pack[row:row + HD, b, a:a + PARTS * (CHUNKS - 1) + 1:PARTS, :]),
                                             words(src[a * HD:(a + 1) * HD, :, b, :])).then_inc(kpacked, 16)
                            sp.dma_start(words(k_pack[row:row + HD, b, HEADS - 1, :]),
                                         words(src[PARTS * HD:PARTS * HD + LASTR, 0:SHARED, b, :])).then_inc(kpacked, 16)
                        sp.dma_start(words(k_pack[MAXROW:MAXROW + 4, b, :, :]), words(marks[:])).then_inc(kpacked, 16)
                    sp.wait_ge(kpacked, 16 * BATCHES * (3 * 4 + 1))
                    sp.wait_ge(ld_vx, 16 * BATCHES)

                @block.tensor
                def _(pe):
                    pe.wait_ge(ld_ctx, 32)
                    pe.wait_ge(ld_wk, 32)
                    pe.wait_ge(ld_wkv, 32)
                    for c in range(CHUNKS):
                        m, at = SIZES[c], STARTS[c]
                        if c >= 2:
                            pe.wait_ge(kraw_enc, c - 1)
                            pe.wait_ge(kraw_vip, c - 1)
                        for kk in range(KC):
                            pe.matmul(ps_a[c % 2][0:m, 0:BATCHES * KEYS], raw["wk"][0:size(kk), kk, at:at + m],
                                      ctx_t[0:size(kk), kk, :, :], start=(kk == 0), stop=(kk == KC - 1))
                        for kk in range(KC):
                            mm = pe.matmul(ps_b[c % 2][0:m, 0:BATCHES * VIP], raw["wkv"][0:size(kk), kk, at:at + m],
                                           ctx_t[0:size(kk), kk, :, ENC:KEYS], start=(kk == 0), stop=(kk == KC - 1))
                        mm.then_inc(k_ps, 1)
                    pe.wait_ge(ld_wv, 32)
                    for b in range(BATCHES):
                        for n in range(2):
                            if 2 * b + n < 2:
                                pe.wait_ge(kraw_enc, 4 + n)
                            else:
                                pe.wait_ge(v_rdy, n + 1)
                            for kk in range(KC):
                                mm = pe.matmul(ps_a[(1 + n) % 2][0:ENC, 0:HALF], ctx_t[0:size(kk), kk, b, 0:ENC],
                                               raw["wv"][0:size(kk), kk, n * HALF:(n + 1) * HALF],
                                               start=(kk == 0), stop=(kk == KC - 1))
                            mm.then_inc(v_ps, 1)
                    pe.wait_ge(ld_wvv, 32)
                    for e in range(KC):
                        for kk in range(KC):
                            mm = pe.matmul(ps_v[0:size(e), e * BATCHES * VIP:(e + 1) * BATCHES * VIP],
                                           raw["wvv"][0:size(kk), kk, e * P:e * P + size(e)],
                                           ctx_t[0:size(kk), kk, :, ENC:KEYS], start=(kk == 0), stop=(kk == KC - 1))
                    mm.then_inc(vv_ps, 1)
                    pe.wait_ge(diag_rdy, 2 * KC)
                    pe.wait_ge(ld_wov, 32)
                    for b in range(BATCHES):
                        for n in range(2):
                            if b == 1:
                                pe.wait_ge(vwlo_rdy, n + 1)
                            for e in range(KC):
                                mm = pe.matmul(ps_w[n][:, 0:HALF], vv_diag[0:size(e), b, e, :, :],
                                               raw["wov"][0:size(e), e, n * HALF:(n + 1) * HALF],
                                               start=(e == 0), stop=(e == KC - 1))
                            mm.then_inc(vw_ps, 1)

                @block.scalar
                def _(act):
                    act.wait_ge(kraw_zero, 1)
                    for c in range(CHUNKS):
                        act.wait_ge(k_ps, c + 1)
                        nc.scalar.copy(k_raw[0:SIZES[c], c, :, ENC:KEYS],
                                       ps_b[c % 2][0:SIZES[c], 0:BATCHES * VIP].rearrange("p (b k) -> p b k", b=BATCHES)).then_inc(kraw_vip, 1)
                    act.wait_ge(kraw_enc, CHUNKS)
                    act.wait_ge(kraw_vip, CHUNKS)
                    nc.scalar.copy(k_hi[:], k_raw[:]).then_inc(khi_rdy, 1)
                    act.wait_ge(ld_small, 64)
                    nc.scalar.copy(marks[:], marks_raw[:, None, :].to_broadcast([4, HEADS, KEYS])).then_inc(krows_rdy, 1)
                    act.wait_ge(vext_zero, 1)
                    act.wait_ge(ld_vx, 16 * BATCHES)
                    for b in range(BATCHES):
                        for n in range(2):
                            act.wait_ge(v_ps, 2 * b + n + 1)
                            nc.scalar.copy(v_ext[0:ENC, b, n * PAIRS:(n + 1) * PAIRS, 0:HD],
                                           ps_a[(1 + n) % 2][0:ENC, 0:HALF].rearrange("p (h d) -> p h d", d=HD)).then_inc(v_rdy, 1)
                    for b in range(BATCHES):
                        for n in range(2):
                            act.wait_ge(vw_ps, 2 * b + n + 1)
                            nc.scalar.copy(vw_hi[:, b, n * HALF:(n + 1) * HALF], ps_w[n][:, 0:HALF]).then_inc(vwhi_rdy, 1)
                    act.wait_ge(ld_wo, 48)
                    nc.scalar.copy(wo_hi[:], raw["wo"][:]).then_inc(wohi_rdy, 1)
                    act.wait_ge(ld_wq, 48)
                    nc.scalar.copy(wq_hi[:], raw["wq"][:]).then_inc(wqhi_rdy, 1)

                @block.vector
                def _(dve):
                    nc.vector.memset(k_raw[:], 0.0).then_inc(kraw_zero, 1)
                    nc.vector.memset(v_ext[:], 0.0).then_inc(vext_zero, 1)
                    dve.wait_ge(kraw_zero, 1)
                    for c in range(CHUNKS):
                        dve.wait_ge(k_ps, c + 1)
                        nc.vector.tensor_copy(k_raw[0:SIZES[c], c, :, 0:ENC],
                                              ps_a[c % 2][0:SIZES[c], 0:BATCHES * KEYS].rearrange("p (b k) -> p b k", b=BATCHES)[:, :, 0:ENC]).then_inc(kraw_enc, 1)
                    dve.wait_ge(khi_rdy, 1)
                    nc.vector.tensor_tensor(k_lo[:], k_raw[:], k_hi[:], ALU.subtract).then_inc(klo_rdy, 1)
                    dve.wait_ge(ld_small, 64)
                    for b in range(BATCHES):
                        for a in range(PARTS):
                            nc.vector.tensor_scalar(k_diag[:, b, :, a, :], k_raw[:, :, b, :], mask_part[0:WIDE, a:a + 1],
                                                    None, ALU.mult)
                    dve.wait_ge(vv_ps, 1)
                    nc.vector.tensor_copy(vv_t[:, 0:FULL], ps_v[:, 0:FULL * BATCHES * VIP].rearrange("p (c b k) -> p c b k", c=FULL, b=BATCHES)).then_inc(vv_rdy, 1)
                    nc.vector.tensor_copy(vv_t[0:REST, FULL], ps_v[0:REST, FULL * BATCHES * VIP:KC * BATCHES * VIP].rearrange("p (b k) -> p b k", b=BATCHES)).then_inc(vv_rdy, 1)
                    dve.wait_ge(vv_rdy, 2)
                    for b in range(BATCHES):
                        for e in range(KC):
                            n = size(e)
                            nc.vector.tensor_tensor(vv_diag[0:n, b, e], vv_t[0:n, e, b, None, :].to_broadcast([n, HEADS, VIP]),
                                                    mask_head[0:n, e, :, None].to_broadcast([n, HEADS, VIP]), ALU.mult).then_inc(diag_rdy, 1)
                    for b in range(BATCHES):
                        for n in range(2):
                            dve.wait_ge(vwhi_rdy, 2 * b + n + 1)
                            nc.vector.tensor_tensor(vw_lo[:, b, n * HALF:(n + 1) * HALF], ps_w[n][:, 0:HALF],
                                                    vw_hi[:, b, n * HALF:(n + 1) * HALF], ALU.subtract).then_inc(vwlo_rdy, 1)
                    dve.wait_ge(wohi_rdy, 1)
                    nc.vector.tensor_tensor(wo_lo[:], raw["wo"][:], wo_hi[:], ALU.subtract)
                    dve.wait_ge(wqhi_rdy, 1)
                    nc.vector.tensor_tensor(wq_lo[:], raw["wq"][:], wq_hi[:], ALU.subtract)

        x_raw = sb("x_raw", [P, BATCHES, KC, TOK])
        x_hi = sb("x_hi", [P, KC, TOK], F32R)
        x_lo = sb("x_lo", [P, FULL, TOK], F32R)
        q_hi = sb("q_hi", [WIDE, CHUNKS, TOK], F32R)
        q_lo = sb("q_lo", [WIDE, CHUNKS, TOK], F32R)
        q_pack = sb("q_pack", [QROWS, BATCHES, HEADS, TOK], F32R)
        neg_max = sb("neg_max", [P, BLK, 2, HEADS])
        nm_hi = sb("nm_hi", [2 * HEADS, TOK], F32R)
        nm_lo = sb("nm_lo", [2 * HEADS, TOK], F32R)
        probs = sb("probs", [P, RING, 2, TOK])
        r_sums = sb("r_sums", [P, BLK, HEADS, 2])
        o_norm = sb("o_norm", [P, BLK, ONW])
        ot_hi = sb("ot_hi", [P, BLK, 6, P], F32R)
        ot_lo = sb("ot_lo", [P, BLK, 6, P], F32R)
        resid = sb("resid", [P, BLK, D])
        y = sb("y", [P, BLK, D])

        x_in = [sem(f"x_in{b}") for b in range(BATCHES)]
        packed = [sem(f"packed{b}") for b in range(BATCHES)]
        max_in = [sem(f"max_in{b}") for b in range(BATCHES)]
        (xhi_rdy, xlo_rdy, q_ps, qhi_rdy, qlo_rdy, guide_ps, guide_max, nmt_ps, nmhi_rdy, nmlo_rdy, s_ps, p_rdy,
         pv_ps, sums_rdy, on_rdy, ot_ps, othi_rdy, otlo_rdy, y_ps, y_rdy, res_in, y_out) = (
            sem(n) for n in ("xhi_rdy", "xlo_rdy", "q_ps", "qhi_rdy", "qlo_rdy", "guide_ps", "guide_max", "nmt_ps",
                             "nmhi_rdy", "nmlo_rdy", "s_ps", "p_rdy", "pv_ps", "sums_rdy", "on_rdy", "ot_ps",
                             "othi_rdy", "otlo_rdy", "y_ps", "y_rdy", "res_in", "y_out"))

        def ps(name, shape):
            return ctx.enter_context(nc.psum_tensor(name, shape, F32))

        s_bank = [ps(f"s_bank{i}", [P, 2, TOK]) for i in range(2)]
        v_bank = [ps(f"v_bank{t}", [P, PAIRS, VCOLS]) for t in range(BLK)]
        q_bank = [ps(f"q_bank{i}", [P, 512]) for i in range(2)]
        o_bank = [ps(f"o_bank{i}", [P, 512]) for i in range(2)]
        block = ctx.enter_context(nc.Block())

        PACKS = 3 * (PARTS + 1)
        MAXES = 4
        JOBS = CHUNKS * BLK
        x_src = dram["xt"]
        r_src = dram["x"].rearrange("b (j t p) e -> b j p t e", t=BLK, p=P)
        y_dst = out.rearrange("b (j t p) e -> b j p t e", t=BLK, p=P)

        def reach(eng, s, count):
            if not (isinstance(count, int) and count <= 0):
                eng.wait_ge(s, count)

        def steps(eng, first_last_and_between):
            first_last_and_between(0, False)
            with eng.Fori(1, STEPS - 1) as j:
                first_last_and_between(j, False)
            first_last_and_between(STEPS - 1, True)

        def next_unit(j, b):
            return (j, 1) if b == 0 else (j + 1, 0)

        def last_unit(j, b):
            return (j, 0) if b == 1 else (j - 1, 1)

        def has_last(j, b):
            return b == 1 or not (isinstance(j, int) and j == 0)

        END = (STEPS - 1, BATCHES - 1)

        @block.sync
        def _(sp):
            def load_x(j, b):
                src = x_src[BATCHES * j + b] if isinstance(j, int) else x_src[bass.ds(BATCHES * j + b, 1)].rearrange("o c n -> (o c) n")
                sp.dma_start(x_raw[:, b, 0:FULL, :], src[0:FULL * P].rearrange("(c p) n -> p c n", p=P)).then_inc(x_in[b], 16)
                for half in range(2):
                    sp.dma_start(x_raw[half * REST:(half + 1) * REST, b, FULL, :], src[FULL * P:D]).then_inc(x_in[b], 16)

            def pack(j, b):
                u = BATCHES * j + b
                sp.wait_ge(qhi_rdy, CHUNKS * (u + 1))
                for row, src in ((0, q_hi), (2 * HD, q_hi), (HD, q_lo)):
                    if row == HD:
                        sp.wait_ge(qlo_rdy, CHUNKS * (u + 1))
                    for a in range(PARTS):
                        sp.dma_start(words(q_pack[row:row + HD, b, a:a + PARTS * (CHUNKS - 1) + 1:PARTS, :]),
                                     words(src[a * HD:(a + 1) * HD, :, :])).then_inc(packed[b], 16)
                    sp.dma_start(words(q_pack[row:row + HD, b, HEADS - 1, :]),
                                 words(src[PARTS * HD:PARTS * HD + LASTR, 0:SHARED, :])).then_inc(packed[b], 16)

            def bring_max(j, b):
                u = BATCHES * j + b
                sp.wait_ge(nmhi_rdy, u + 1)
                sp.wait_ge(nmlo_rdy, u + 1)
                for r in range(4):
                    src, g = (nm_hi, nm_lo)[r // 2], r % 2
                    sp.dma_start(words(q_pack[MAXROW + r:MAXROW + r + 1, b, :, :]),
                                 words(src[g * HEADS:(g + 1) * HEADS, :])).then_inc(max_in[b], 16)

            def load_residual(j, b):
                reach(sp, y_rdy, 4 * (BATCHES * j + b))
                src = r_src[b, j] if isinstance(j, int) else r_src[b, bass.ds(j, 1)].rearrange("o p t e -> (o p) t e")
                sp.dma_start(resid[:], src).then_inc(res_in, 16)

            def store(j, b):
                sp.wait_ge(y_rdy, 4 * (BATCHES * j + b + 1))
                dst = y_dst[b, j] if isinstance(j, int) else y_dst[b, bass.ds(j, 1)].rearrange("o p t e -> (o p) t e")
                sp.dma_start(dst, y[:]).then_inc(y_out, 16)

            def unit(j, b, last):
                u = BATCHES * j + b
                if not last:
                    sp.wait_ge(xlo_rdy, u + 1)
                    load_x(j + 1, b)
                if has_last(j, b):
                    load_residual(*last_unit(j, b))
                nj, nb = next_unit(j, b)
                if not (last and b == 1):
                    pack(nj, nb)
                    bring_max(nj, nb)
                if has_last(j, b):
                    store(*last_unit(j, b))

            for b in range(BATCHES):
                load_x(0, b)
            pack(0, 0)
            bring_max(0, 0)

            def step(j, last):
                for b in range(BATCHES):
                    unit(j, b, last)
            steps(sp, step)
            load_residual(*END)
            store(*END)
            sp.wait_ge(y_out, 16 * BATCHES * STEPS)

        @block.tensor
        def _(pe):
            def queries(j, b, c):
                u = BATCHES * j + b
                if c == 0:
                    sp_wait = xlo_rdy
                    pe.wait_ge(sp_wait, u + 1)
                if c < 2:
                    reach(pe, guide_max, JOBS * u)
                else:
                    pe.wait_ge(qlo_rdy, CHUNKS * u + c - 1)
                m, at, bank = SIZES[c], STARTS[c], q_bank[c % 2]
                terms = []
                for kk in range(FULL):
                    terms += [(wq_hi, x_hi, kk, P), (wq_hi, x_lo, kk, P), (wq_lo, x_hi, kk, P)]
                terms += [(wq_hi, x_hi, FULL, P), (wq_lo, x_hi, FULL, REST)]
                for n, (w, x, kk, k) in enumerate(terms):
                    mm = pe.matmul(bank[0:m, 0:TOK], w[0:k, kk, at:at + m], x[0:k, kk, :],
                                   start=(n == 0), stop=(n == len(terms) - 1))
                mm.then_inc(q_ps, 1)

            def guide(j, b, i):
                u = BATCHES * j + b
                c, t = i // BLK, i % BLK
                if i == 0:
                    pe.wait_ge(qhi_rdy, CHUNKS * (u + 1))
                if i < 2:
                    pe.wait_ge(qlo_rdy, CHUNKS * u + 4 + i)
                else:
                    pe.wait_ge(guide_max, JOBS * u + i - 1)
                bank = q_bank[(i + 1) % 2]
                mm = pe.matmul(bank[:, 0:PARTS * KEYS], q_hi[0:SIZES[c], c, t * P:(t + 1) * P],
                               k_diag[0:SIZES[c], b, c, :, :], start=True, stop=True)
                if c == CHUNKS - 1:
                    pe.wait_ge(packed[b], 16 * PACKS * (j + 1))
                    mm = pe.matmul(bank[:, PARTS * KEYS:512], q_pack[0:MAXROW, b, HEADS - 1, t * P:(t + 1) * P],
                                   k_pack[0:MAXROW, b, HEADS - 1, :], start=True, stop=True)
                mm.then_inc(guide_ps, 1)

            def turn_max(j, b):
                u = BATCHES * j + b
                pe.wait_ge(guide_max, JOBS * (u + 1))
                reach(pe, p_rdy, PAIRS * u - 1)
                for t in range(BLK):
                    mm = pe.transpose(s_bank[0][0:2 * HEADS, 0, t * P:(t + 1) * P],
                                      neg_max[:, t].rearrange("p g h -> p (g h)"), ident[:])
                mm.then_inc(nmt_ps, 1)

            def scores(j, b, k):
                u = BATCHES * j + b
                if k == 0:
                    pe.wait_ge(packed[b], 16 * PACKS * (j + 1))
                    pe.wait_ge(max_in[b], 16 * MAXES * (j + 1))
                reach(pe, p_rdy, PAIRS * u + k - 1)
                for a in range(2):
                    mm = pe.matmul(s_bank[k % 2][:, a, :], k_pack[:, b, 2 * k + a, :], q_pack[:, b, 2 * k + a, :],
                                   start=True, stop=True)
                mm.then_inc(s_ps, 1)

            def values(j, b, k):
                u = BATCHES * j + b
                pe.wait_ge(p_rdy, PAIRS * u + k + 1)
                if k % (PAIRS // 2) == 0:
                    reach(pe, on_rdy, 2 * BLK * u + BLK * (k // (PAIRS // 2)))
                for t in range(BLK):
                    for a in range(2):
                        h = 2 * k + a
                        mm = pe.matmul(v_bank[t][:, h % PAIRS, :], probs[:, k % RING, a, t * P:(t + 1) * P],
                                       v_ext[:, b, h, :], start=True, stop=True)
                mm.then_inc(pv_ps, 1)

            def turn_o(j, b, t):
                u = BATCHES * j + b
                pe.wait_ge(on_rdy, 2 * BLK * u + BLK + t + 1)
                for half, chunks in enumerate((range(4), range(4, 6))):
                    if t == 0:
                        reach(pe, y_rdy, 4 * u - 1 + half)
                    else:
                        pe.wait_ge(otlo_rdy, 4 * u + 1 + half)
                    for c in chunks:
                        mm = pe.transpose(o_bank[half][:, (c % 4) * P:(c % 4 + 1) * P],
                                          o_norm[:, t, c * P:(c + 1) * P], ident[:])
                    mm.then_inc(ot_ps, 1)

            def output(j, b, t, n):
                u = BATCHES * j + b
                if t == 0:
                    pe.wait_ge(otlo_rdy, 4 * u + 3 + n)
                else:
                    pe.wait_ge(y_rdy, 4 * u + 1 + n)
                cols = slice(n * HALF, (n + 1) * HALF)
                terms = []
                for c in range(FULL):
                    terms += [(ot_hi, wo_hi[:, c, cols], c, P), (ot_lo, wo_hi[:, c, cols], c, P), (ot_hi, wo_lo[:, c, cols], c, P)]
                terms += [(ot_hi, wo_hi[:, FULL, cols], FULL, P), (ot_hi, wo_lo[0:REST, FULL, cols], FULL, REST)]
                terms += [(ot_hi, vw_hi[:, b, cols], 5, P), (ot_lo, vw_hi[:, b, cols], 5, P), (ot_hi, vw_lo[:, b, cols], 5, P)]
                for i, (o, w, c, k) in enumerate(terms):
                    mm = pe.matmul(o_bank[n][:, 0:HALF], o[0:k, t, c, :], w, start=(i == 0), stop=(i == len(terms) - 1))
                mm.then_inc(y_ps, 1)

            def unit(j, b, last):
                nj, nb = next_unit(j, b)
                more, before = not (last and b == 1), has_last(j, b)
                for k in range(PAIRS):
                    if more and k == 0:
                        queries(nj, nb, 0)
                    scores(j, b, k)
                    if before and k == 0:
                        turn_o(*last_unit(j, b), 1)
                    if more and 0 < k < CHUNKS:
                        queries(nj, nb, k)
                    g = k - CHUNKS
                    if more and g >= 0:
                        guide(nj, nb, 4 * g)
                        guide(nj, nb, 4 * g + 1)
                    if before and g >= 0:
                        output(*last_unit(j, b), g // 2, g % 2)
                    if more and 0 <= g < 2:
                        guide(nj, nb, 4 * g + 2)
                        guide(nj, nb, 4 * g + 3)
                    if k >= 1:
                        values(j, b, k - 1)
                if more:
                    turn_max(nj, nb)
                values(j, b, PAIRS - 1)
                if before:
                    output(*last_unit(j, b), 1, 1)
                turn_o(j, b, 0)

            for c in range(CHUNKS):
                queries(0, 0, c)
            for i in range(JOBS):
                guide(0, 0, i)
            turn_max(0, 0)

            def step(j, last):
                for b in range(BATCHES):
                    unit(j, b, last)
            steps(pe, step)
            turn_o(*END, 1)
            for t in range(BLK):
                for n in range(2):
                    output(*END, t, n)

        @block.scalar
        def _(act):
            def split_x(j, b):
                u = BATCHES * j + b
                act.wait_ge(x_in[b], 48 * (j + 1))
                reach(act, q_ps, CHUNKS * u)
                nc.scalar.copy(x_hi[:], x_raw[:, b]).then_inc(xhi_rdy, 1)

            def queries(j, b, c):
                u = BATCHES * j + b
                act.wait_ge(q_ps, CHUNKS * u + c + 1)
                if c == 0:
                    reach(act, guide_ps, JOBS * u)
                    reach(act, packed[1 - b], 16 * PACKS * (j + b))
                nc.scalar.copy(q_hi[0:SIZES[c], c, :], q_bank[c % 2][0:SIZES[c], 0:TOK]).then_inc(qhi_rdy, 1)

            def split_max(j, b):
                u = BATCHES * j + b
                act.wait_ge(nmt_ps, u + 1)
                reach(act, max_in[1 - b], 16 * MAXES * (j + b))
                nc.scalar.copy(nm_hi[:], s_bank[0][0:2 * HEADS, 0, :]).then_inc(nmhi_rdy, 1)

            def exponentials(j, b, k):
                u = BATCHES * j + b
                act.wait_ge(s_ps, PAIRS * u + k + 1)
                reach(act, pv_ps, PAIRS * u + k + 1 - RING)
                nc.scalar.activation(probs[:, k % RING], s_bank[k % 2][:], ACT.Exp, scale=SCALE).then_inc(p_rdy, 1)

            def turned(j, b, t, half):
                u = BATCHES * j + b
                act.wait_ge(ot_ps, 4 * u + 2 * t + half + 1)
                reach(act, y_ps, 4 * u - 2 + 2 * t)
                a, z = (0, 4) if half == 0 else (4, 6)
                nc.scalar.copy(ot_hi[:, t, a:z], o_bank[half][:, 0:(z - a) * P].rearrange("p (c n) -> p c n", n=P)).then_inc(othi_rdy, 1)

            def unit(j, b, last):
                nj, nb = next_unit(j, b)
                more = not (last and b == 1)
                for k in range(PAIRS):
                    if more and k == 0:
                        queries(nj, nb, 0)
                    exponentials(j, b, k)
                    if has_last(j, b) and k == 0:
                        turned(*last_unit(j, b), 1, 0)
                        turned(*last_unit(j, b), 1, 1)
                    if more and 0 < k < CHUNKS:
                        queries(nj, nb, k)
                    if not last and k == CHUNKS:
                        split_x(j + 1, b)
                if more:
                    split_max(nj, nb)
                turned(j, b, 0, 0)
                turned(j, b, 0, 1)

            split_x(0, 0)
            for c in range(CHUNKS):
                queries(0, 0, c)
            split_x(0, 1)
            split_max(0, 0)

            def step(j, last):
                for b in range(BATCHES):
                    unit(j, b, last)
            steps(act, step)
            turned(*END, 1, 0)
            turned(*END, 1, 1)

        @block.vector
        def _(dve):
            def split_x(j, b):
                u = BATCHES * j + b
                dve.wait_ge(xhi_rdy, u + 1)
                nc.vector.tensor_tensor(x_lo[:], x_raw[:, b, 0:FULL], x_hi[:, 0:FULL], ALU.subtract)
                nc.vector.tensor_tensor(x_hi[REST:P, FULL], x_raw[REST:P, b, FULL], x_hi[REST:P, FULL],
                                        ALU.subtract).then_inc(xlo_rdy, 1)

            def queries(j, b, c):
                u = BATCHES * j + b
                dve.wait_ge(qhi_rdy, CHUNKS * u + c + 1)
                nc.vector.tensor_tensor(q_lo[0:SIZES[c], c, :], q_bank[c % 2][0:SIZES[c], 0:TOK], q_hi[0:SIZES[c], c, :],
                                        ALU.subtract).then_inc(qlo_rdy, 1)

            def maximum(j, b, i):
                u = BATCHES * j + b
                c, t = i // BLK, i % BLK
                dve.wait_ge(guide_ps, JOBS * u + i + 1)
                if i == 0:
                    reach(dve, nmt_ps, u)
                heads = PARTS + (c == CHUNKS - 1)
                bank = q_bank[(i + 1) % 2][:, 0:heads * KEYS].rearrange("p (h k) -> p h k", k=KEYS)
                h = PARTS * c
                nc.vector.reduce_max(neg_max[:, t, 0, h:h + heads], bank[:, :, 0:ENC], AX.X, negate=True)
                nc.vector.reduce_max(neg_max[:, t, 1, h:h + heads], bank[:, :, ENC:KEYS], AX.X, negate=True).then_inc(guide_max, 1)

            def split_max(j, b):
                u = BATCHES * j + b
                dve.wait_ge(nmhi_rdy, u + 1)
                nc.vector.tensor_tensor(nm_lo[:], s_bank[0][0:2 * HEADS, 0, :], nm_hi[:], ALU.subtract).then_inc(nmlo_rdy, 1)

            def divide(j, b, half, t):
                u = BATCHES * j + b
                n = 2 * BLK * u + BLK * half + t
                h0, hz = half * PAIRS, (half + 1) * PAIRS
                if t == 0:
                    dve.wait_ge(pv_ps, PAIRS * u + (half + 1) * PAIRS // 2)
                if half == 0 and t == 0:
                    reach(dve, ot_ps, 4 * u)
                bank = v_bank[t]
                nc.vector.reciprocal(r_sums[:, t, h0:hz, :], bank[:, :, HD + VIP:HD + VIP + 2]).then_inc(sums_rdy, 1)
                dve.wait_ge(sums_rdy, n + 1)
                enc = r_sums[:, t, h0:hz, 0:1]
                vip = r_sums[:, t, h0:hz, 1:2]
                nc.vector.tensor_tensor(o_norm[:, t, 0:ONB].rearrange("p (h d) -> p h d", d=32)[:, h0:hz], bank[:, :, 0:32],
                                        enc.to_broadcast([P, PAIRS, 32]), ALU.mult)
                for copy in range(2):
                    at = ONB + copy * HEADS * TAIL
                    nc.vector.tensor_tensor(o_norm[:, t, at:at + HEADS * TAIL].rearrange("p (h d) -> p h d", d=TAIL)[:, h0:hz],
                                            bank[:, :, 32:HD], enc.to_broadcast([P, PAIRS, TAIL]), ALU.mult)
                nc.vector.tensor_tensor(o_norm[:, t, VIPCOL:ONW].rearrange("p (h k) -> p h k", k=VIP)[:, h0:hz],
                                        bank[:, :, HD:HD + VIP], vip.to_broadcast([P, PAIRS, VIP]), ALU.mult).then_inc(on_rdy, 1)

            def turned(j, b, t, half):
                u = BATCHES * j + b
                dve.wait_ge(othi_rdy, 4 * u + 2 * t + half + 1)
                if half == 0:
                    nc.vector.tensor_tensor(ot_lo[:, t, 0:4], o_bank[0][:].rearrange("p (c n) -> p c n", n=P),
                                            ot_hi[:, t, 0:4], ALU.subtract).then_inc(otlo_rdy, 1)
                else:
                    nc.vector.tensor_tensor(ot_lo[:, t, 5], o_bank[1][:, P:2 * P], ot_hi[:, t, 5], ALU.subtract)
                    nc.vector.tensor_tensor(ot_hi[REST:P, t, 4], o_bank[1][REST:P, 0:P], ot_hi[REST:P, t, 4],
                                            ALU.subtract).then_inc(otlo_rdy, 1)

            def output(j, b, t, n):
                u = BATCHES * j + b
                dve.wait_ge(y_ps, 4 * u + 2 * t + n + 1)
                if t == 0 and n == 0:
                    dve.wait_ge(res_in, 16 * (u + 1))
                    reach(dve, y_out, 16 * u)
                cols = slice(n * HALF, (n + 1) * HALF)
                nc.vector.tensor_tensor(y[:, t, cols], o_bank[n][:, 0:HALF], resid[:, t, cols], ALU.add).then_inc(y_rdy, 1)

            def unit(j, b, last):
                nj, nb = next_unit(j, b)
                more = not (last and b == 1)
                before = has_last(j, b)
                for k in range(PAIRS):
                    if more and k < CHUNKS:
                        queries(nj, nb, k)
                    if before and k == 0:
                        turned(*last_unit(j, b), 1, 0)
                        turned(*last_unit(j, b), 1, 1)
                    if k == PAIRS // 2:
                        for t in range(BLK):
                            divide(j, b, 0, t)
                    g = k - CHUNKS
                    if more and g >= 0:
                        maximum(nj, nb, 4 * g)
                        maximum(nj, nb, 4 * g + 1)
                    if before and g >= 0:
                        output(*last_unit(j, b), g // 2, g % 2)
                    if more and 0 <= g < 2:
                        maximum(nj, nb, 4 * g + 2)
                        maximum(nj, nb, 4 * g + 3)
                    if not last and g == 1:
                        split_x(j + 1, b)
                if more:
                    split_max(nj, nb)
                divide(j, b, 1, 0)
                divide(j, b, 1, 1)
                if before:
                    output(*last_unit(j, b), 1, 1)
                turned(j, b, 0, 0)
                turned(j, b, 0, 1)

            split_x(0, 0)
            for c in range(CHUNKS):
                queries(0, 0, c)
            for i in range(JOBS):
                maximum(0, 0, i)
            split_max(0, 0)
            split_x(0, 1)

            def step(j, last):
                for b in range(BATCHES):
                    unit(j, b, last)
            steps(dve, step)
            turned(*END, 1, 0)
            turned(*END, 1, 1)
            for t in range(BLK):
                for n in range(2):
                    output(*END, t, n)


def kernel(x, ctx_1152, L0_xattn_Wq, L0_xattn_Wk, L0_xattn_Wv, L0_xattn_Wo, L0_xattn_Wk_vip, L0_xattn_Wv_vip,
           L0_xattn_Wo_vip):
    import concourse.bacc as bacc
    from concourse.bass_utils import run_bass_kernel_spmd

    x, ctx = np.asarray(x), np.asarray(ctx_1152)
    B, S, D = x.shape
    keys = ctx.shape[1]
    hd = D // HEADS
    order, _ = channel_order(hd)
    enc = (keys - NUM_VIP) % keys
    vip = keys - enc
    c = np.ascontiguousarray

    def turned(w, rows=slice(None), cols=slice(None)):
        return c(np.asarray(w).T[rows][:, cols])

    mask_part = np.zeros((P, PARTS), np.float32)
    for a in range(PARTS):
        mask_part[a * hd:(a + 1) * hd, a] = 1
    mask_head = np.zeros((P, D // P + 1, HEADS), np.float32)
    for e in range(D):
        mask_head[e % P, e // P, e // hd] = 1
    marks = np.zeros((4, keys), np.float32)
    marks[0::2, :enc] = 1
    marks[1::2, enc:] = 1
    v_const = np.zeros((keys, HEADS, VCOLS - hd), np.float32)
    for k in range(vip):
        v_const[enc + k, :, k] = 1
    v_const[:enc, :, vip] = 1
    v_const[enc:, :, vip + 1] = 1
    arrays = {
        "x": c(x),
        "xt": c(x.reshape(B, S // TOK, TOK, D).transpose(1, 0, 3, 2).reshape(B * S // TOK, D, TOK)),
        "ctx": c(ctx.transpose(2, 0, 1).reshape(D, B * keys)),
        "wq": turned(L0_xattn_Wq, cols=order),
        "wk": turned(L0_xattn_Wk, cols=order),
        "wkv": turned(L0_xattn_Wk_vip, cols=order),
        "wv": turned(L0_xattn_Wv),
        "wvv": turned(L0_xattn_Wv_vip),
        "wo": turned(L0_xattn_Wo, rows=output_order(hd)),
        "wov": turned(L0_xattn_Wo_vip),
        "mask_part": mask_part, "mask_head": mask_head, "marks": marks, "v_const": v_const,
        "ident": np.eye(P, dtype=np.float32),
    }
    nc = bacc.Bacc("TRN2", target_bir_lowering=False, num_devices=1)
    dram = {n: nc.dram_tensor(f"in_{n}", a.shape, F32, kind="ExternalInput").ap() for n, a in arrays.items()}
    out = nc.dram_tensor("out", (B, S, D), F32, kind="ExternalOutput").ap()
    build(nc, dram, out)
    r = run_bass_kernel_spmd(nc, [{f"in_{n}": a for n, a in arrays.items()}], core_ids=[0])
    return r.results[0]["out"]
```

```python
from contextlib import ExitStack

import numpy as np

import concourse.bass as bass
from concourse import mybir

F32 = mybir.dt.float32
F32R = mybir.dt.float32r
ALU = mybir.AluOpType
ACT = mybir.ActivationFunctionType
AX = mybir.AxisListType

NUM_VIP = 136
HEADS = 16
P = 128
TOK = 256
BLK = TOK // P
BATCHES = 2
PARTS = 3
CHUNKS = 5
SHARED = 4
VCOLS = 64


def channel_order(head_dim):
    order, sizes = [], []
    for c in range(CHUNKS):
        rows = [head_dim * (PARTS * c + a) + d for a in range(PARTS) for d in range(head_dim)]
        if c < SHARED:
            rows += [head_dim * (HEADS - 1) + SHARED * r + c for r in range(head_dim // SHARED)]
        order += rows
        sizes.append(len(rows))
    return order, sizes


def output_order(head_dim):
    main = [head_dim * h + d for h in range(HEADS) for d in range(32)]
    return main + [head_dim * h + d for h in range(HEADS) for d in range(32, head_dim)]


def build(nc, dram, out):
    D = dram["wq"].shape[0]
    S = dram["x"].shape[1]
    HD = D // HEADS
    KEYS = dram["ctx"].shape[1] // BATCHES
    ENC = (KEYS - NUM_VIP) % KEYS
    VIP = KEYS - ENC
    STEPS = S // TOK
    FULL = D // P
    REST = D - FULL * P
    KC = FULL + 1
    HALF = D // 2
    SCALE = float(HD) ** -0.5
    _, SIZES = channel_order(HD)
    STARTS = [sum(SIZES[:c]) for c in range(CHUNKS)]
    WIDE = max(SIZES)
    LASTR = HD // SHARED
    QROWS = 3 * HD + 4
    MAXROW = 3 * HD
    TAIL = HD - 32
    ONB = HEADS * 32
    VIPCOL = ONB + 2 * HEADS * TAIL
    ONW = VIPCOL + HEADS * VIP
    PAIRS = HEADS // 2
    RING = 3
    assert REST == 64 == HEADS * TAIL and ONW == 6 * P and KEYS == P and HEADS * VIP == P
    assert HD + VIP + 2 <= VCOLS and QROWS <= P and sum(SIZES) == D

    def words(ap):
        return ap.bitcast(F32)

    with ExitStack() as ctx:
        def sem(name):
            return ctx.enter_context(nc.semaphore(name))

        def sb(name, shape, dt=F32, stack=ctx):
            return stack.enter_context(nc.sbuf_tensor(name, shape, dt))

        wq_hi = sb("wq_hi", [P, KC, D], F32R)
        wq_lo = sb("wq_lo", [P, KC, D], F32R)
        wo_hi = sb("wo_hi", [P, KC, D], F32R)
        wo_lo = sb("wo_lo", [P, KC, D], F32R)
        vw_hi = sb("vw_hi", [P, BATCHES, D], F32R)
        vw_lo = sb("vw_lo", [P, BATCHES, D], F32R)
        k_diag = sb("k_diag", [WIDE, BATCHES, CHUNKS, PARTS, KEYS], F32R)
        k_pack = sb("k_pack", [QROWS, HEADS, BATCHES, KEYS], F32R)
        v_ext = sb("v_ext", [KEYS, BATCHES, HEADS, VCOLS])
        ident = sb("ident", [P, P])
        x_raw = sb("x_raw", [P, BATCHES, KC, TOK])
        x_hi = sb("x_hi", [P, KC, TOK], F32R)
        x_lo = sb("x_lo", [P, FULL, TOK], F32R)
        q_hi = sb("q_hi", [WIDE, CHUNKS, TOK], F32R)
        q_lo = sb("q_lo", [WIDE, CHUNKS, TOK], F32R)
        q_pack = sb("q_pack", [WIDE, BATCHES, HEADS, TOK], F32R)
        k_hi = q_pack[:, 1, 0:CHUNKS, :]
        k_lo = q_pack[:, 1, CHUNKS:2 * CHUNKS, :]
        neg_max = sb("neg_max", [P, BLK, 2, HEADS])
        nm_hi = sb("nm_hi", [2 * HEADS, TOK], F32R)
        nm_lo = sb("nm_lo", [2 * HEADS, TOK], F32R)
        r_sums = sb("r_sums", [P, BLK, HEADS, 2])
        with ExitStack() as early:
            def st(name, shape, dt=F32):
                return sb(name, shape, dt, early)

            raw_a = st("raw_a", [P, KC, D])
            ctx_t = st("ctx_t", [P, KC, BATCHES * KEYS])
            k_raw = st("k_raw", [WIDE, CHUNKS, BATCHES, KEYS])
            raw_c = st("raw_c", [P, KC, D])
            vv_t = st("vv_t", [P, KC, BATCHES, VIP])
            vv_diag = st("vv_diag", [P, BATCHES, KC, HEADS, VIP])
            vip_raw = vv_diag[0:BATCHES * VIP].rearrange("p b c h k -> p (b c h k)")[:, 0:D]
            raw_b = st("raw_b", [P, KC, D])
            mask_part = st("mask_part", [P, PARTS])
            mask_head = st("mask_head", [P, KC, HEADS])
            marks_raw = st("marks_raw", [4, KEYS])
            marks = st("marks", [4, KEYS], F32R)
            v_const = st("v_const", [KEYS, VCOLS - HD])
        probs = sb("probs", [P, RING, 2, TOK])
        o_norm = sb("o_norm", [P, BLK, ONW])
        ot_hi = sb("ot_hi", [P, BLK, 6, P], F32R)
        ot_lo = sb("ot_lo", [P, BLK, 6, P], F32R)
        resid = sb("resid", [P, BLK, D])
        y = sb("y", [P, BLK, D])

        ld_keys = [sem(f"ld_keys{kk}") for kk in range(KC)]
        (ld_ident, ld_wkv, ld_wv, ld_wvv, ld_wov, ld_wo, ld_wq, ld_small, vext_zero, vext_const, ktext_ps, ktext_rdy,
         kvip_ps, kvip_raw, kvip_turned, kraw_rdy, khi_rdy, klo_rdy, marks_rdy, kpacked, kdiag0_rdy, kdiag1_rdy,
         kraw_zero, v_ps, v_rdy, vvip_ps, vvip_raw, vvip_turned, vv_rdy, diag_rdy, vw_ps, vwhi_rdy, vwlo_rdy, wqhi_rdy,
         wqlo_rdy, wohi_rdy, wolo_rdy) = (
            sem(n) for n in ("ld_ident", "ld_wkv", "ld_wv", "ld_wvv", "ld_wov", "ld_wo", "ld_wq", "ld_small",
                             "vext_zero", "vext_const", "ktext_ps", "ktext_rdy", "kvip_ps", "kvip_raw", "kvip_turned",
                             "kraw_rdy", "khi_rdy", "klo_rdy", "marks_rdy", "kpacked", "kdiag0_rdy", "kdiag1_rdy",
                             "kraw_zero", "v_ps", "v_rdy", "vvip_ps", "vvip_raw", "vvip_turned", "vv_rdy",
                             "diag_rdy", "vw_ps", "vwhi_rdy", "vwlo_rdy", "wqhi_rdy", "wqlo_rdy", "wohi_rdy",
                             "wolo_rdy"))
        x_in = [sem(f"x_in{b}") for b in range(BATCHES)]
        packed = [sem(f"packed{b}") for b in range(BATCHES)]
        last_packed = [sem(f"last_packed{b}") for b in range(BATCHES)]
        max_in = [sem(f"max_in{b}") for b in range(BATCHES)]
        (xhi_rdy, xlo_main, xlo_rdy, q_ps, qhi_rdy, qlo_rdy, guide_ps, guide_max, nmt_ps, nmhi_rdy, nmlo_rdy, s_ps, p_rdy,
         pv_ps, sums_rdy, on_rdy, ot_ps, othi_rdy, otlo_rdy, y_ps, y_rdy, res_in, y_out) = (
            sem(n) for n in ("xhi_rdy", "xlo_main", "xlo_rdy", "q_ps", "qhi_rdy", "qlo_rdy", "guide_ps", "guide_max", "nmt_ps",
                             "nmhi_rdy", "nmlo_rdy", "s_ps", "p_rdy", "pv_ps", "sums_rdy", "on_rdy", "ot_ps",
                             "othi_rdy", "otlo_rdy", "y_ps", "y_rdy", "res_in", "y_out"))

        def ps(name, shape):
            return ctx.enter_context(nc.psum_tensor(name, shape, F32))

        s_bank = [ps(f"s_bank{i}", [P, 2, TOK]) for i in range(2)]
        v_bank = [ps(f"v_bank{t}", [P, PAIRS, VCOLS]) for t in range(BLK)]
        q_bank = [ps(f"q_bank{i}", [P, 512]) for i in range(2)]
        o_bank = [ps(f"o_bank{i}", [P, 512]) for i in range(2)]
        v_flat = [bank[:].rearrange("p h n -> p (h n)") for bank in v_bank]
        s_flat = [bank[:].rearrange("p a n -> p (a n)") for bank in s_bank]
        key_bank = [q_bank[0], q_bank[1], o_bank[0], o_bank[1], v_flat[0]]
        kvip_bank = [v_flat[1], s_flat[0]]
        value_bank = [o_bank[0][:], o_bank[1][:], s_flat[0], s_flat[1]]
        block = ctx.enter_context(nc.Block())

        def size(kk):
            return P if kk < FULL else REST

        SMALLS = 4
        KPACKS = 3 * (PARTS + 1) + 1
        PACKS = 3 * PARTS
        MAXES = 2
        WQ_PIECES = ((0, 2), (2, 4), (4, KC))
        JOBS = CHUNKS * BLK
        x_src = dram["xt"]
        r_src = dram["x"].rearrange("b (j t p) e -> b j p t e", t=BLK, p=P)
        y_dst = out.rearrange("b (j t p) e -> b j p t e", t=BLK, p=P)

        def reach(eng, s, count):
            if not (isinstance(count, int) and count <= 0):
                eng.wait_ge(s, count)

        def steps(eng, step):
            step(0, False)
            with eng.Fori(1, STEPS - 1) as j:
                step(j, False)
            step(STEPS - 1, True)

        def next_unit(j, b):
            return (j, 1) if b == 0 else (j + 1, 0)

        def last_unit(j, b):
            return (j, 0) if b == 1 else (j - 1, 1)

        def has_last(j, b):
            return b == 1 or not (isinstance(j, int) and j == 0)

        END = (STEPS - 1, BATCHES - 1)

        @block.sync
        def _(sp):
            def load_x(j, b):
                src = x_src[BATCHES * j + b] if isinstance(j, int) else x_src[bass.ds(BATCHES * j + b, 1)].rearrange("o c n -> (o c) n")
                sp.dma_start(x_raw[:, b, 0:FULL, :], src[0:FULL * P].rearrange("(c p) n -> p c n", p=P)).then_inc(x_in[b], 16)
                for half in range(2):
                    sp.dma_start(x_raw[half * REST:(half + 1) * REST, b, FULL, :], src[FULL * P:D]).then_inc(x_in[b], 16)

            def pack(j, b):
                u = BATCHES * j + b
                sp.wait_ge(qhi_rdy, CHUNKS * u + SHARED)
                sp.wait_ge(qlo_rdy, CHUNKS * u + SHARED)
                for row, src in ((0, q_hi), (2 * HD, q_hi), (HD, q_lo)):
                    sp.dma_start(words(q_pack[row:row + HD, b, HEADS - 1, :]),
                                 words(src[PARTS * HD:PARTS * HD + LASTR, 0:SHARED, :])).then_inc(last_packed[b], 16)
                sp.wait_ge(qhi_rdy, CHUNKS * (u + 1))
                sp.wait_ge(qlo_rdy, CHUNKS * (u + 1))
                for row, src in ((0, q_hi), (2 * HD, q_hi), (HD, q_lo)):
                    for a in range(PARTS):
                        sp.dma_start(words(q_pack[row:row + HD, b, a:a + PARTS * (CHUNKS - 1) + 1:PARTS, :]),
                                     words(src[a * HD:(a + 1) * HD, :, :])).then_inc(packed[b], 16)

            def bring_max(j, b):
                u = BATCHES * j + b
                sp.wait_ge(nmhi_rdy, u + 1)
                sp.dma_start(words(q_pack[MAXROW:MAXROW + 2, b, :, :]), words(nm_hi[:])).then_inc(max_in[b], 16)
                sp.wait_ge(nmlo_rdy, u + 1)
                sp.dma_start(words(q_pack[MAXROW + 2:MAXROW + 4, b, :, :]), words(nm_lo[:])).then_inc(max_in[b], 16)

            def load_residual(j, b):
                if isinstance(j, int) and j == 0 and b == 0:
                    sp.wait_ge(wolo_rdy, 1)
                reach(sp, y_rdy, 4 * (BATCHES * j + b))
                src = r_src[b, j] if isinstance(j, int) else r_src[b, bass.ds(j, 1)].rearrange("o p t e -> (o p) t e")
                sp.dma_start(resid[:], src).then_inc(res_in, 16)

            def store(j, b):
                sp.wait_ge(y_rdy, 4 * (BATCHES * j + b + 1))
                dst = y_dst[b, j] if isinstance(j, int) else y_dst[b, bass.ds(j, 1)].rearrange("o p t e -> (o p) t e")
                sp.dma_start(dst, y[:]).then_inc(y_out, 16)

            def unit(j, b, last):
                u = BATCHES * j + b
                if not last:
                    sp.wait_ge(xlo_rdy, u + 1)
                    load_x(j + 1, b)
                if has_last(j, b):
                    load_residual(*last_unit(j, b))
                nj, nb = next_unit(j, b)
                if not (last and b == 1):
                    pack(nj, nb)
                    bring_max(nj, nb)
                if has_last(j, b):
                    store(*last_unit(j, b))

            def load(name, dst, landed, twice=False):
                w = dram[name]
                sp.dma_start(dst[:, 0:FULL, :], w[0:FULL * P, :].rearrange("(c p) n -> p c n", p=P)).then_inc(landed, 16)
                for half in range(1 + twice):
                    sp.dma_start(dst[half * REST:(half + 1) * REST, FULL, :], w[FULL * P:D, :]).then_inc(landed, 16)

            for kk in range(KC):
                rows, at = size(kk), kk * P
                sp.dma_start(ctx_t[0:rows, kk], dram["ctx"][at:at + rows, :]).then_inc(ld_keys[kk], 16)
                sp.dma_start(raw_a[0:rows, kk], dram["wk"][at:at + rows, :]).then_inc(ld_keys[kk], 16)
            load("wkv", raw_b, ld_wkv)
            sp.dma_start(ident[:], dram["ident"]).then_inc(ld_ident, 16)
            load_x(0, 0)
            load("wq", raw_c, ld_wq, twice=True)
            sp.dma_start(mask_part[:], dram["mask_part"]).then_inc(ld_small, 16)
            sp.dma_start(mask_head[:], dram["mask_head"]).then_inc(ld_small, 16)
            sp.dma_start(marks_raw[:], dram["marks"]).then_inc(ld_small, 16)
            sp.dma_start(v_const[:], dram["v_const"]).then_inc(ld_small, 16)
            sp.wait_ge(wqhi_rdy, len(WQ_PIECES))
            sp.wait_ge(wqlo_rdy, len(WQ_PIECES))
            load("wv", raw_c, ld_wv)
            sp.wait_ge(ktext_ps, CHUNKS)
            load("wvv", raw_a, ld_wvv)
            load_x(0, 1)
            sp.wait_ge(khi_rdy, 1)
            sp.wait_ge(klo_rdy, 1)
            for row, src in ((0, k_hi), (HD, k_hi), (2 * HD, k_lo)):
                for a in range(PARTS):
                    sp.dma_start(words(k_pack[row:row + HD, a:a + PARTS * (CHUNKS - 1) + 1:PARTS].rearrange("p h b k -> p h (b k)")),
                                 words(src[a * HD:(a + 1) * HD, :, :])).then_inc(kpacked, 16)
                sp.dma_start(words(k_pack[row:row + HD, HEADS - 1].rearrange("p b k -> p (b k)")),
                             words(src[PARTS * HD:PARTS * HD + LASTR, 0:SHARED, :])).then_inc(kpacked, 16)
            sp.wait_ge(marks_rdy, 1)
            sp.dma_start(words(k_pack[MAXROW:MAXROW + 4].rearrange("p h b k -> p (h b) k")),
                         words(marks[:])[:, None, :].to_broadcast([4, HEADS * BATCHES, KEYS])).then_inc(kpacked, 16)
            pack(0, 0)
            bring_max(0, 0)
            load("wov", raw_b, ld_wov)
            sp.wait_ge(v_ps, 4)
            load("wo", raw_c, ld_wo, twice=True)

            def step(j, last):
                for b in range(BATCHES):
                    unit(j, b, last)
            steps(sp, step)
            load_residual(*END)
            store(*END)
            sp.wait_ge(y_out, 16 * BATCHES * STEPS)

        @block.tensor
        def _(pe):
            def queries(j, b, c):
                u = BATCHES * j + b
                if c == 0:
                    pe.wait_ge(xlo_rdy, u + 1)
                if c < 2:
                    reach(pe, guide_max, JOBS * u)
                else:
                    pe.wait_ge(qlo_rdy, CHUNKS * u + c - 1)
                m, at, bank = SIZES[c], STARTS[c], q_bank[c % 2]
                terms = []
                for kk in range(FULL):
                    terms += [(wq_hi, x_hi, kk, P), (wq_hi, x_lo, kk, P), (wq_lo, x_hi, kk, P)]
                terms += [(wq_hi, x_hi, FULL, P), (wq_lo, x_hi, FULL, REST)]
                for n, (w, x, kk, k) in enumerate(terms):
                    mm = pe.matmul(bank[0:m, 0:TOK], w[0:k, kk, at:at + m], x[0:k, kk, :],
                                   start=(n == 0), stop=(n == len(terms) - 1))
                mm.then_inc(q_ps, 1)

            def guide(j, b, i):
                u = BATCHES * j + b
                c, t = i // BLK, i % BLK
                if i < 2:
                    pe.wait_ge(qlo_rdy, CHUNKS * u + 4 + i)
                else:
                    pe.wait_ge(guide_max, JOBS * u + i - 1)
                bank = q_bank[(i + 1) % 2]
                mm = pe.matmul(bank[:, 0:PARTS * KEYS], q_hi[0:SIZES[c], c, t * P:(t + 1) * P],
                               k_diag[0:SIZES[c], b, c, :, :], start=True, stop=True)
                if c == CHUNKS - 1:
                    pe.wait_ge(last_packed[b], 16 * 3 * (j + 1))
                    mm = pe.matmul(bank[:, PARTS * KEYS:512], q_pack[0:MAXROW, b, HEADS - 1, t * P:(t + 1) * P],
                                   k_pack[0:MAXROW, HEADS - 1, b, :], start=True, stop=True)
                mm.then_inc(guide_ps, 1)

            def turn_max(j, b):
                u = BATCHES * j + b
                pe.wait_ge(guide_max, JOBS * (u + 1))
                reach(pe, p_rdy, PAIRS * u - 1)
                for t in range(BLK):
                    mm = pe.transpose(s_bank[0][0:2 * HEADS, 0, t * P:(t + 1) * P],
                                      neg_max[:, t].rearrange("p g h -> p (g h)"), ident[:])
                mm.then_inc(nmt_ps, 1)

            def scores(j, b, k):
                u = BATCHES * j + b
                if k == 0:
                    pe.wait_ge(packed[b], 16 * PACKS * (j + 1))
                    pe.wait_ge(max_in[b], 16 * MAXES * (j + 1))
                reach(pe, p_rdy, PAIRS * u + k - 1)
                for a in range(2):
                    mm = pe.matmul(s_bank[k % 2][:, a, :], k_pack[:, 2 * k + a, b, :], q_pack[0:QROWS, b, 2 * k + a, :],
                                   start=True, stop=True)
                mm.then_inc(s_ps, 1)

            def values(j, b, k):
                u = BATCHES * j + b
                pe.wait_ge(p_rdy, PAIRS * u + k + 1)
                if k % (PAIRS // 2) == 0:
                    reach(pe, on_rdy, 2 * BLK * u + BLK * (k // (PAIRS // 2)))
                for t in range(BLK):
                    for a in range(2):
                        h = 2 * k + a
                        mm = pe.matmul(v_bank[t][:, h % PAIRS, :], probs[:, k % RING, a, t * P:(t + 1) * P],
                                       v_ext[:, b, h, :], start=True, stop=True)
                mm.then_inc(pv_ps, 1)

            def turn_o(j, b, t):
                u = BATCHES * j + b
                pe.wait_ge(on_rdy, 2 * BLK * u + BLK + t + 1)
                for half, chunks in enumerate((range(4), range(4, 6))):
                    if isinstance(u, int) and u == 0 and t == 0:
                        pe.wait_ge(vwlo_rdy, 3 + half)
                    elif t == 0:
                        reach(pe, y_rdy, 4 * u - 1 + half)
                    else:
                        pe.wait_ge(otlo_rdy, 4 * u + 1 + half)
                    for c in chunks:
                        mm = pe.transpose(o_bank[half][:, (c % 4) * P:(c % 4 + 1) * P],
                                          o_norm[:, t, c * P:(c + 1) * P], ident[:])
                    mm.then_inc(ot_ps, 1)

            def output(j, b, t, n, between=None):
                u = BATCHES * j + b
                if isinstance(u, int) and u == 0 and t == 0 and n == 0:
                    pe.wait_ge(wolo_rdy, 1)
                    pe.wait_ge(vwlo_rdy, 4)
                if t == 0:
                    pe.wait_ge(otlo_rdy, 4 * u + 3 + n)
                else:
                    pe.wait_ge(y_rdy, 4 * u + 1 + n)
                cols = slice(n * HALF, (n + 1) * HALF)
                terms = []
                for c in range(FULL):
                    terms += [(ot_hi, wo_hi[:, c, cols], c, P), (ot_lo, wo_hi[:, c, cols], c, P), (ot_hi, wo_lo[:, c, cols], c, P)]
                terms += [(ot_hi, wo_hi[:, FULL, cols], FULL, P), (ot_hi, wo_lo[0:REST, FULL, cols], FULL, REST)]
                terms += [(ot_hi, vw_hi[:, b, cols], 5, P), (ot_lo, vw_hi[:, b, cols], 5, P), (ot_hi, vw_lo[:, b, cols], 5, P)]
                for i, (o, w, c, k) in enumerate(terms):
                    mm = pe.matmul(o_bank[n][:, 0:HALF], o[0:k, t, c, :], w, start=(i == 0), stop=(i == len(terms) - 1))
                    if between is not None and i == len(terms) // 2:
                        between()
                mm.then_inc(y_ps, 1)

            def unit(j, b, last):
                nj, nb = next_unit(j, b)
                more, before = not (last and b == 1), has_last(j, b)

                def last_output(g, between=None):
                    if before:
                        output(*last_unit(j, b), g // 2, g % 2, between)
                    else:
                        vip_weights(g // 2, g % 2)
                        if between is not None:
                            between()

                def last_turn(t):
                    if before:
                        turn_o(*last_unit(j, b), t)

                def next_queries(c):
                    if more:
                        queries(nj, nb, c)

                def next_guide(i):
                    if more:
                        guide(nj, nb, i)

                next_queries(0)
                last_turn(0)
                scores(j, b, 0)
                scores(j, b, 1)
                next_queries(1)
                values(j, b, 0)
                last_turn(1)
                values(j, b, 1)
                for k in (2, 3):
                    scores(j, b, k)
                    next_queries(k)
                    values(j, b, k)
                scores(j, b, 4)
                next_queries(4)
                scores(j, b, 5)
                if more and b == 0 and isinstance(j, int) and j == 0:
                    pe.wait_ge(kdiag1_rdy, PARTS)
                next_guide(0)
                last_output(0)
                next_guide(1)
                next_guide(2)
                values(j, b, 4)
                next_guide(3)
                scores(j, b, 6)
                next_guide(4)
                values(j, b, 5)
                next_guide(5)
                last_output(1, between=lambda: next_guide(6))
                next_guide(7)
                next_guide(8)
                scores(j, b, 7)
                values(j, b, 6)
                next_guide(9)
                values(j, b, 7)
                if more:
                    turn_max(nj, nb)
                last_output(2)
                last_output(3)

            def text_keys(c, kk):
                m, at = SIZES[c], STARTS[c]
                mm = pe.matmul(key_bank[c][0:m, 0:BATCHES * ENC], raw_a[0:size(kk), kk, at:at + m],
                               ctx_t[0:size(kk), kk, 0:BATCHES * ENC], start=(kk == 0), stop=(kk == KC - 1))
                if kk == KC - 1:
                    mm.then_inc(ktext_ps, 1)

            def vip_rows(bank, w, n, made):
                for kk in range(KC):
                    mm = pe.matmul(bank[0:BATCHES * VIP, 0:HALF], ctx_t[0:size(kk), kk, BATCHES * ENC:],
                                   w[0:size(kk), kk, n * HALF:(n + 1) * HALF], start=(kk == 0), stop=(kk == KC - 1))
                mm.then_inc(made, 1)

            def turn_vip(bank, chunks, turned):
                n = BATCHES * VIP
                for i, (at, m) in enumerate(chunks):
                    mm = pe.transpose(bank[0:m, i * n:(i + 1) * n], vip_raw[:, at:at + m], ident[0:n, 0:n])
                mm.then_inc(turned, 1)

            def text_values(b, n):
                for kk in range(KC):
                    mm = pe.matmul(value_bank[2 * b + n][0:ENC, 0:HALF], ctx_t[0:size(kk), kk, b * ENC:(b + 1) * ENC],
                                   raw_c[0:size(kk), kk, n * HALF:(n + 1) * HALF], start=(kk == 0), stop=(kk == KC - 1))
                mm.then_inc(v_ps, 1)

            def vip_weights(b, n):
                if b == 0 and n == 0:
                    pe.wait_ge(diag_rdy, BATCHES * KC)
                    pe.wait_ge(ld_wov, 32)
                    pe.wait_ge(v_rdy, 2)
                if b == 1:
                    pe.wait_ge(vwlo_rdy, n + 1)
                for e in range(KC):
                    mm = pe.matmul(o_bank[n][:, 0:HALF], vv_diag[0:size(e), b, e, :, :],
                                   raw_b[0:size(e), e, n * HALF:(n + 1) * HALF], start=(e == 0), stop=(e == KC - 1))
                mm.then_inc(vw_ps, 1)

            for kk in range(KC):
                pe.wait_ge(ld_keys[kk], 32)
                for c in range(CHUNKS):
                    text_keys(c, kk)
            pe.wait_ge(ld_wkv, 32)
            for n in range(2):
                vip_rows(kvip_bank[n], raw_b, n, kvip_ps)
            pe.wait_ge(ld_ident, 16)
            pe.wait_ge(kvip_raw, 2)
            turn_vip(s_flat[1], list(zip(STARTS, SIZES)), kvip_turned)
            pe.wait_ge(wqlo_rdy, len(WQ_PIECES))
            pe.wait_ge(ktext_rdy, CHUNKS)
            for c in range(CHUNKS):
                queries(0, 0, c)
            pe.wait_ge(kdiag0_rdy, PARTS)
            pe.wait_ge(ld_wv, 32)
            for i in range(4):
                guide(0, 0, 2 * i)
                guide(0, 0, 2 * i + 1)
                text_values(i // 2, i % 2)
            pe.wait_ge(kpacked, 16 * KPACKS)
            guide(0, 0, 8)
            guide(0, 0, 9)
            pe.wait_ge(ld_wvv, 32)
            vip_rows(v_flat[0], raw_a, 0, vvip_ps)
            pe.wait_ge(v_rdy, 3)
            turn_max(0, 0)
            vip_rows(v_flat[1], raw_a, 1, vvip_ps)
            pe.wait_ge(vvip_raw, 2)
            turn_vip(v_flat[0], [(e * P, size(e)) for e in range(KC)], vvip_turned)
            pe.wait_ge(v_rdy, 4)
            pe.wait_ge(vext_const, 1)
            pe.wait_ge(vv_rdy, 2)

            def step(j, last):
                for b in range(BATCHES):
                    unit(j, b, last)
            steps(pe, step)
            for t in range(BLK):
                turn_o(*END, t)
            for t in range(BLK):
                for n in range(2):
                    output(*END, t, n)

        @block.gpsimd
        def _(pool):
            def split_x(j, b):
                u = BATCHES * j + b
                pool.wait_ge(xhi_rdy, u + 1)
                nc.gpsimd.tensor_tensor(x_lo[:], x_raw[:, b, 0:FULL], x_hi[:, 0:FULL], ALU.subtract).then_inc(xlo_main, 1)
                pool.wait_ge(xlo_main, u + 1)
                nc.gpsimd.tensor_tensor(x_hi[REST:P, FULL], x_raw[REST:P, b, FULL], x_hi[REST:P, FULL],
                                        ALU.subtract).then_inc(xlo_rdy, 1)
                pool.wait_ge(xlo_rdy, u + 1)

            nc.gpsimd.memset(v_ext[:], 0.0).then_inc(vext_zero, 1)
            split_x(0, 0)
            pool.wait_ge(ld_small, 16 * SMALLS)
            pool.wait_ge(vext_zero, 1)
            nc.gpsimd.tensor_copy(v_ext[:, :, :, HD:VCOLS].rearrange("p b h n -> p (b h) n"),
                                  v_const[:, None, :].to_broadcast([KEYS, BATCHES * HEADS, VCOLS - HD])).then_inc(vext_const, 1)
            pool.wait_ge(kraw_rdy, 1)
            for a in range(PARTS):
                nc.gpsimd.tensor_scalar(k_diag[:, 1, :, a, :], k_raw[:, :, 1, :], mask_part[0:WIDE, a:a + 1],
                                        None, ALU.mult).then_inc(kdiag1_rdy, 1)
            split_x(0, 1)
            pool.wait_ge(vv_rdy, 2)
            for b in range(BATCHES):
                for e in range(KC):
                    m = size(e)
                    nc.gpsimd.tensor_tensor(vv_diag[0:m, b, e], vv_t[0:m, e, b, None, :].to_broadcast([m, HEADS, VIP]),
                                            mask_head[0:m, e, :, None].to_broadcast([m, HEADS, VIP]), ALU.mult).then_inc(diag_rdy, 1)
            pool.wait_ge(wohi_rdy, 1)
            nc.gpsimd.tensor_tensor(wo_lo[:], raw_c[:], wo_hi[:], ALU.subtract).then_inc(wolo_rdy, 1)

            def step(j, last):
                for b in range(BATCHES):
                    if not last:
                        split_x(j + 1, b)
            steps(pool, step)

        @block.scalar
        def _(act):
            def split_x(j, b):
                u = BATCHES * j + b
                act.wait_ge(x_in[b], 48 * (j + 1))
                reach(act, q_ps, CHUNKS * u)
                nc.scalar.copy(x_hi[:], x_raw[:, b]).then_inc(xhi_rdy, 1)

            def queries(j, b, c):
                u = BATCHES * j + b
                act.wait_ge(q_ps, CHUNKS * u + c + 1)
                if c == 0:
                    reach(act, guide_ps, JOBS * u)
                    reach(act, packed[1 - b], 16 * PACKS * (j + b))
                nc.scalar.copy(q_hi[0:SIZES[c], c, :], q_bank[c % 2][0:SIZES[c], 0:TOK]).then_inc(qhi_rdy, 1)

            def split_max(j, b):
                u = BATCHES * j + b
                act.wait_ge(nmt_ps, u + 1)
                reach(act, max_in[1 - b], 16 * MAXES * (j + b))
                nc.scalar.copy(nm_hi[:], s_bank[0][0:2 * HEADS, 0, :]).then_inc(nmhi_rdy, 1)

            def exponentials(j, b, k):
                u = BATCHES * j + b
                act.wait_ge(s_ps, PAIRS * u + k + 1)
                reach(act, pv_ps, PAIRS * u + k + 1 - RING)
                nc.scalar.activation(probs[:, k % RING], s_bank[k % 2][:], ACT.Exp, scale=SCALE).then_inc(p_rdy, 1)

            def turned(j, b, t, half):
                u = BATCHES * j + b
                act.wait_ge(ot_ps, 4 * u + 2 * t + half + 1)
                reach(act, y_ps, 4 * u - 2 + 2 * t)
                a, z = (0, 4) if half == 0 else (4, 6)
                nc.scalar.copy(ot_hi[:, t, a:z], o_bank[half][:, 0:(z - a) * P].rearrange("p (c n) -> p c n", n=P)).then_inc(othi_rdy, 1)

            def vip_weights(b, n):
                act.wait_ge(vw_ps, 2 * b + n + 1)
                nc.scalar.copy(vw_hi[:, b, n * HALF:(n + 1) * HALF], o_bank[n][:, 0:HALF]).then_inc(vwhi_rdy, 1)

            def unit(j, b, last):
                nj, nb = next_unit(j, b)
                more = not (last and b == 1)
                before = has_last(j, b)

                def next_queries(c):
                    if more:
                        queries(nj, nb, c)

                def last_turned(t):
                    if before:
                        turned(*last_unit(j, b), t, 0)
                        turned(*last_unit(j, b), t, 1)

                next_queries(0)
                last_turned(0)
                exponentials(j, b, 0)
                exponentials(j, b, 1)
                next_queries(1)
                last_turned(1)
                for k in (2, 3, 4):
                    exponentials(j, b, k)
                    next_queries(k)
                exponentials(j, b, 5)
                if not last:
                    split_x(j + 1, b)
                if not before:
                    act.wait_ge(ld_wo, 48)
                    nc.scalar.copy(wo_hi[:], raw_c[:]).then_inc(wohi_rdy, 1)
                    vip_weights(0, 0)
                exponentials(j, b, 6)
                if not before:
                    vip_weights(0, 1)
                exponentials(j, b, 7)
                if not before:
                    vip_weights(1, 0)
                if more:
                    split_max(nj, nb)
                if not before:
                    vip_weights(1, 1)
                    act.wait_ge(wolo_rdy, 1)

            split_x(0, 0)
            act.wait_ge(ld_wq, 48)
            for lo, hi in WQ_PIECES:
                nc.scalar.copy(wq_hi[:, lo:hi], raw_c[:, lo:hi]).then_inc(wqhi_rdy, 1)
            act.wait_ge(kraw_rdy, 1)
            nc.scalar.copy(k_hi, k_raw[:].rearrange("p c b k -> p c (b k)")).then_inc(khi_rdy, 1)
            act.wait_ge(ld_small, 16 * SMALLS)
            nc.scalar.copy(marks[:], marks_raw[:]).then_inc(marks_rdy, 1)
            for c in range(CHUNKS):
                queries(0, 0, c)
            act.wait_ge(vext_zero, 1)
            for b in range(BATCHES):
                for n in range(2):
                    act.wait_ge(v_ps, 2 * b + n + 1)
                    nc.scalar.copy(v_ext[0:ENC, b, n * PAIRS:(n + 1) * PAIRS, 0:HD],
                                   value_bank[2 * b + n][0:ENC, 0:HALF].rearrange("p (h d) -> p h d", d=HD)).then_inc(v_rdy, 1)
                    if b == 0 and n == 1:
                        split_x(0, 1)
            split_max(0, 0)

            def step(j, last):
                for b in range(BATCHES):
                    unit(j, b, last)
            steps(act, step)
            for t in range(BLK):
                turned(*END, t, 0)
                turned(*END, t, 1)

        @block.vector
        def _(dve):
            def queries(j, b, c):
                u = BATCHES * j + b
                dve.wait_ge(qhi_rdy, CHUNKS * u + c + 1)
                nc.vector.tensor_tensor(q_lo[0:SIZES[c], c, :], q_bank[c % 2][0:SIZES[c], 0:TOK], q_hi[0:SIZES[c], c, :],
                                        ALU.subtract).then_inc(qlo_rdy, 1)

            def maximum(j, b, i):
                u = BATCHES * j + b
                c, t = i // BLK, i % BLK
                dve.wait_ge(guide_ps, JOBS * u + i + 1)
                if i == 0:
                    reach(dve, nmt_ps, u)
                heads = PARTS + (c == CHUNKS - 1)
                bank = q_bank[(i + 1) % 2][:, 0:heads * KEYS].rearrange("p (h k) -> p h k", k=KEYS)
                h = PARTS * c
                nc.vector.reduce_max(neg_max[:, t, 0, h:h + heads], bank[:, :, 0:ENC], AX.X, negate=True)
                nc.vector.reduce_max(neg_max[:, t, 1, h:h + heads], bank[:, :, ENC:KEYS], AX.X, negate=True).then_inc(guide_max, 1)

            def split_max(j, b):
                u = BATCHES * j + b
                dve.wait_ge(nmhi_rdy, u + 1)
                nc.vector.tensor_tensor(nm_lo[:], s_bank[0][0:2 * HEADS, 0, :], nm_hi[:], ALU.subtract).then_inc(nmlo_rdy, 1)

            def divide(j, b, half, t):
                u = BATCHES * j + b
                n = 2 * BLK * u + BLK * half + t
                h0, hz = half * PAIRS, (half + 1) * PAIRS
                if t == 0:
                    dve.wait_ge(pv_ps, PAIRS * u + (half + 1) * PAIRS // 2)
                if half == 0 and t == 0:
                    reach(dve, ot_ps, 4 * u)
                bank = v_bank[t]
                nc.vector.reciprocal(r_sums[:, t, h0:hz, :], bank[:, :, HD + VIP:HD + VIP + 2]).then_inc(sums_rdy, 1)
                dve.wait_ge(sums_rdy, n + 1)
                enc = r_sums[:, t, h0:hz, 0:1]
                vip = r_sums[:, t, h0:hz, 1:2]
                nc.vector.tensor_tensor(o_norm[:, t, 0:ONB].rearrange("p (h d) -> p h d", d=32)[:, h0:hz], bank[:, :, 0:32],
                                        enc.to_broadcast([P, PAIRS, 32]), ALU.mult)
                for copy in range(2):
                    at = ONB + copy * HEADS * TAIL
                    nc.vector.tensor_tensor(o_norm[:, t, at:at + HEADS * TAIL].rearrange("p (h d) -> p h d", d=TAIL)[:, h0:hz],
                                            bank[:, :, 32:HD], enc.to_broadcast([P, PAIRS, TAIL]), ALU.mult)
                nc.vector.tensor_tensor(o_norm[:, t, VIPCOL:ONW].rearrange("p (h k) -> p h k", k=VIP)[:, h0:hz],
                                        bank[:, :, HD:HD + VIP], vip.to_broadcast([P, PAIRS, VIP]), ALU.mult).then_inc(on_rdy, 1)

            def turned(j, b, t, half):
                u = BATCHES * j + b
                dve.wait_ge(othi_rdy, 4 * u + 2 * t + half + 1)
                if half == 0:
                    nc.vector.tensor_tensor(ot_lo[:, t, 0:4], o_bank[0][:].rearrange("p (c n) -> p c n", n=P),
                                            ot_hi[:, t, 0:4], ALU.subtract).then_inc(otlo_rdy, 1)
                else:
                    nc.vector.tensor_tensor(ot_lo[:, t, 5], o_bank[1][:, P:2 * P], ot_hi[:, t, 5], ALU.subtract)
                    nc.vector.tensor_tensor(ot_hi[REST:P, t, 4], o_bank[1][REST:P, 0:P], ot_hi[REST:P, t, 4],
                                            ALU.subtract).then_inc(otlo_rdy, 1)

            def output(j, b, t, n):
                u = BATCHES * j + b
                dve.wait_ge(y_ps, 4 * u + 2 * t + n + 1)
                if t == 0 and n == 0:
                    dve.wait_ge(res_in, 16 * (u + 1))
                    reach(dve, y_out, 16 * u)
                cols = slice(n * HALF, (n + 1) * HALF)
                nc.vector.tensor_tensor(y[:, t, cols], o_bank[n][:, 0:HALF], resid[:, t, cols], ALU.add).then_inc(y_rdy, 1)

            def unit(j, b, last):
                nj, nb = next_unit(j, b)
                more = not (last and b == 1)
                before = has_last(j, b)

                def last_output(g):
                    if before:
                        output(*last_unit(j, b), g // 2, g % 2)
                    else:
                        vip_weights(g // 2, g % 2)

                def next_maximum(i):
                    if more:
                        maximum(nj, nb, i)

                for k in range(CHUNKS):
                    if more:
                        queries(nj, nb, k)
                    if before and k < BLK:
                        turned(*last_unit(j, b), k, 0)
                        turned(*last_unit(j, b), k, 1)
                    if k == 3:
                        for t in range(BLK):
                            divide(j, b, 0, t)
                next_maximum(0)
                last_output(0)
                for i in range(1, 7):
                    next_maximum(i)
                last_output(1)
                for i in range(7, JOBS):
                    next_maximum(i)
                divide(j, b, 1, 0)
                if more:
                    split_max(nj, nb)
                divide(j, b, 1, 1)
                last_output(2)
                last_output(3)

            def text_keys(c):
                dve.wait_ge(ktext_ps, c + 1)
                nc.vector.tensor_copy(k_raw[0:SIZES[c], c, :, 0:ENC],
                                      key_bank[c][0:SIZES[c], 0:BATCHES * ENC].rearrange("p (b k) -> p b k", b=BATCHES)).then_inc(ktext_rdy, 1)

            def vip_rows(bank, n, made, copied):
                dve.wait_ge(made, n + 1)
                nc.vector.tensor_copy(vip_raw[:, n * HALF:(n + 1) * HALF], bank[0:BATCHES * VIP, 0:HALF]).then_inc(copied, 1)

            def vip_keys():
                dve.wait_ge(kvip_turned, 1)
                n = BATCHES * VIP
                for c0, c1 in ((0, CHUNKS - 1), (CHUNKS - 1, CHUNKS)):
                    m = SIZES[c0]
                    copy = nc.vector.tensor_copy(k_raw[0:m, c0:c1, :, ENC:KEYS],
                                                 s_flat[1][0:m, c0 * n:c1 * n].rearrange("p (c b k) -> p c b k", b=BATCHES, k=VIP))
                copy.then_inc(kraw_rdy, 1)

            def split_wq(i):
                dve.wait_ge(wqhi_rdy, i + 1)
                lo, hi = WQ_PIECES[i]
                nc.vector.tensor_tensor(wq_lo[:, lo:hi], raw_c[:, lo:hi], wq_hi[:, lo:hi], ALU.subtract).then_inc(wqlo_rdy, 1)

            def vip_weights(b, n):
                dve.wait_ge(vwhi_rdy, 2 * b + n + 1)
                nc.vector.tensor_tensor(vw_lo[:, b, n * HALF:(n + 1) * HALF], o_bank[n][:, 0:HALF],
                                        vw_hi[:, b, n * HALF:(n + 1) * HALF], ALU.subtract).then_inc(vwlo_rdy, 1)

            nc.vector.memset(k_raw[:, CHUNKS - 1], 0.0).then_inc(kraw_zero, 1)
            dve.wait_ge(kraw_zero, 1)
            for c in range(CHUNKS):
                text_keys(c)
            for n in range(2):
                vip_rows(kvip_bank[n], n, kvip_ps, kvip_raw)
            split_wq(0)
            vip_keys()
            split_wq(1)
            split_wq(2)
            dve.wait_ge(khi_rdy, 1)
            nc.vector.tensor_tensor(k_lo, k_raw[:].rearrange("p c b k -> p c (b k)"), k_hi, ALU.subtract).then_inc(klo_rdy, 1)
            dve.wait_ge(ld_small, 16 * SMALLS)
            for c in range(CHUNKS):
                queries(0, 0, c)
                if c < PARTS:
                    nc.vector.tensor_scalar(k_diag[:, 0, :, c, :], k_raw[:, :, 0, :], mask_part[0:WIDE, c:c + 1],
                                            None, ALU.mult).then_inc(kdiag0_rdy, 1)
            for i in range(JOBS):
                maximum(0, 0, i)
            vip_rows(v_flat[0], 0, vvip_ps, vvip_raw)
            split_max(0, 0)
            vip_rows(v_flat[1], 1, vvip_ps, vvip_raw)
            dve.wait_ge(vvip_turned, 1)
            n = FULL * BATCHES * VIP
            nc.vector.tensor_copy(vv_t[:, 0:FULL], v_flat[0][:, 0:n].rearrange("p (c b k) -> p c b k", c=FULL, b=BATCHES)).then_inc(vv_rdy, 1)
            nc.vector.tensor_copy(vv_t[0:REST, FULL], v_flat[0][0:REST, n:n + BATCHES * VIP].rearrange("p (b k) -> p b k", b=BATCHES)).then_inc(vv_rdy, 1)

            def step(j, last):
                for b in range(BATCHES):
                    unit(j, b, last)
            steps(dve, step)
            for t in range(BLK):
                turned(*END, t, 0)
                turned(*END, t, 1)
            for t in range(BLK):
                for n in range(2):
                    output(*END, t, n)


def kernel(x, ctx_1152, L0_xattn_Wq, L0_xattn_Wk, L0_xattn_Wv, L0_xattn_Wo, L0_xattn_Wk_vip, L0_xattn_Wv_vip,
           L0_xattn_Wo_vip):
    import concourse.bacc as bacc
    from concourse.bass_utils import run_bass_kernel_spmd

    x, ctx = np.asarray(x), np.asarray(ctx_1152)
    B, S, D = x.shape
    keys = ctx.shape[1]
    hd = D // HEADS
    order, _ = channel_order(hd)
    enc = (keys - NUM_VIP) % keys
    vip = keys - enc
    c = np.ascontiguousarray

    def turned(w, rows=slice(None), cols=slice(None)):
        return c(np.asarray(w).T[rows][:, cols])

    mask_part = np.zeros((P, PARTS), np.float32)
    for a in range(PARTS):
        mask_part[a * hd:(a + 1) * hd, a] = 1
    mask_head = np.zeros((P, D // P + 1, HEADS), np.float32)
    for e in range(D):
        mask_head[e % P, e // P, e // hd] = 1
    marks = np.zeros((4, keys), np.float32)
    marks[0::2, :enc] = 1
    marks[1::2, enc:] = 1
    v_const = np.zeros((keys, VCOLS - hd), np.float32)
    for k in range(vip):
        v_const[enc + k, k] = 1
    v_const[:enc, vip] = 1
    v_const[enc:, vip + 1] = 1
    arrays = {
        "x": c(x),
        "xt": c(x.reshape(B, S // TOK, TOK, D).transpose(1, 0, 3, 2).reshape(B * S // TOK, D, TOK)),
        "ctx": c(np.concatenate([ctx[:, :enc].reshape(B * enc, D), ctx[:, enc:].reshape(B * vip, D)]).T),
        "wq": turned(L0_xattn_Wq, cols=order),
        "wk": turned(L0_xattn_Wk, cols=order),
        "wkv": turned(L0_xattn_Wk_vip, cols=order),
        "wv": turned(L0_xattn_Wv),
        "wvv": turned(L0_xattn_Wv_vip),
        "wo": turned(L0_xattn_Wo, rows=output_order(hd)),
        "wov": turned(L0_xattn_Wo_vip),
        "mask_part": mask_part, "mask_head": mask_head, "marks": marks, "v_const": v_const,
        "ident": np.eye(P, dtype=np.float32),
    }
    nc = bacc.Bacc("TRN2", target_bir_lowering=False, num_devices=1)
    dram = {n: nc.dram_tensor(f"in_{n}", a.shape, F32, kind="ExternalInput").ap() for n, a in arrays.items()}
    out = nc.dram_tensor("out", (B, S, D), F32, kind="ExternalOutput").ap()
    build(nc, dram, out)
    r = run_bass_kernel_spmd(nc, [{f"in_{n}": a for n, a in arrays.items()}], core_ids=[0])
    return r.results[0]["out"]
```

```python
from contextlib import ExitStack

import numpy as np

import concourse.bass as bass
from concourse import mybir

F32 = mybir.dt.float32
F32R = mybir.dt.float32r
ALU = mybir.AluOpType
ACT = mybir.ActivationFunctionType
AX = mybir.AxisListType

NUM_VIP = 136
HEADS = 16
P = 128
TOK = 256
BLK = TOK // P
BATCHES = 2
PARTS = 3
CHUNKS = 5
SHARED = 4
VCOLS = 64


def channel_order(head_dim):
    order, sizes = [], []
    for c in range(CHUNKS):
        rows = [head_dim * (PARTS * c + a) + d for a in range(PARTS) for d in range(head_dim)]
        if c < SHARED:
            rows += [head_dim * (HEADS - 1) + SHARED * r + c for r in range(head_dim // SHARED)]
        order += rows
        sizes.append(len(rows))
    return order, sizes


def output_order(head_dim):
    main = [head_dim * h + d for h in range(HEADS) for d in range(32)]
    return main + [head_dim * h + d for h in range(HEADS) for d in range(32, head_dim)]


def build(nc, dram, out):
    D = dram["wq"].shape[0]
    S = dram["x"].shape[1]
    HD = D // HEADS
    KEYS = dram["ctx"].shape[1] // BATCHES
    ENC = (KEYS - NUM_VIP) % KEYS
    VIP = KEYS - ENC
    STEPS = S // TOK
    FULL = D // P
    REST = D - FULL * P
    KC = FULL + 1
    HALF = D // 2
    SCALE = float(HD) ** -0.5
    _, SIZES = channel_order(HD)
    STARTS = [sum(SIZES[:c]) for c in range(CHUNKS)]
    WIDE = max(SIZES)
    LASTR = HD // SHARED
    QROWS = 3 * HD + 4
    MAXROW = 3 * HD
    TAIL = HD - 32
    ONB = HEADS * 32
    VIPCOL = ONB + 2 * HEADS * TAIL
    ONW = VIPCOL + HEADS * VIP
    PAIRS = HEADS // 2
    RING = 3
    VW_PARTS = [list(range(g * HALF // P, ((g + 1) * HALF - 1) // P + 1)) for g in range(2)]
    VW_AT = [0, len(VW_PARTS[0])]
    VROWS = PAIRS * VIP
    assert REST == 64 == HEADS * TAIL and ONW == 6 * P and KEYS == P and HEADS * VIP == P
    assert 2 * VROWS == P and PAIRS * 2 == HEADS
    assert HD + VIP + 2 <= VCOLS and QROWS <= P and sum(SIZES) == D

    def words(ap):
        return ap.bitcast(F32)

    with ExitStack() as ctx:
        def sem(name):
            return ctx.enter_context(nc.semaphore(name))

        def sb(name, shape, dt=F32, stack=ctx):
            return stack.enter_context(nc.sbuf_tensor(name, shape, dt))

        wq_hi = sb("wq_hi", [P, KC, D], F32R)
        wq_lo = sb("wq_lo", [P, KC, D], F32R)
        wo_hi = sb("wo_hi", [P, KC, D], F32R)
        wo_lo = sb("wo_lo", [P, KC, D], F32R)
        vw_hi = sb("vw_hi", [P, BATCHES, D], F32R)
        vw_lo = sb("vw_lo", [P, BATCHES, D], F32R)
        k_diag = sb("k_diag", [WIDE, BATCHES, CHUNKS, PARTS, KEYS], F32R)
        k_pack = sb("k_pack", [QROWS, HEADS, BATCHES, KEYS], F32R)
        v_ext = sb("v_ext", [KEYS, BATCHES, HEADS, VCOLS])
        ident = sb("ident", [P, P])
        x_raw = sb("x_raw", [P, BATCHES, KC, TOK])
        x_hi = sb("x_hi", [P, KC, TOK], F32R)
        x_lo = sb("x_lo", [P, FULL, TOK], F32R)
        q_hi = sb("q_hi", [WIDE, CHUNKS, TOK], F32R)
        q_lo = sb("q_lo", [WIDE, CHUNKS, TOK], F32R)
        q_pack = sb("q_pack", [WIDE, BATCHES, HEADS, TOK], F32R)
        k_hi = q_pack[:, 1, 0:CHUNKS, :]
        k_lo = q_pack[:, 1, CHUNKS:2 * CHUNKS, :]
        neg_max = sb("neg_max", [P, BLK, 2, HEADS])
        nm_hi = sb("nm_hi", [2 * HEADS, TOK], F32R)
        nm_lo = sb("nm_lo", [2 * HEADS, TOK], F32R)
        r_sums = sb("r_sums", [P, BLK, HEADS, 2])
        with ExitStack() as early:
            def st(name, shape, dt=F32):
                return sb(name, shape, dt, early)

            raw_a = st("raw_a", [P, KC, D])
            ctx_t = st("ctx_t", [P, KC, BATCHES * KEYS])
            k_raw = st("k_raw", [WIDE, CHUNKS, BATCHES, KEYS])
            vv_t = st("vv_t", [P, KC, BATCHES, VIP])
            raw_b = st("raw_b", [P, KC, D])
            raw_c = st("raw_c", [P, KC, D])
            vv_diag = st("vv_diag", [P, sum(map(len, VW_PARTS)), BATCHES, PAIRS, VIP])
            vip_raw = vv_diag[0:BATCHES * VIP].rearrange("p b c h k -> p (b c h k)")[:, 0:D]
            mask_part = st("mask_part", [P, PARTS])
            mask_head = st("mask_head", [P, KC, HEADS])
            marks_raw = st("marks_raw", [4, KEYS])
            marks = st("marks", [4, KEYS], F32R)
            v_const = st("v_const", [KEYS, VCOLS - HD])
        probs = sb("probs", [P, RING, 2, TOK])
        o_norm = sb("o_norm", [P, BLK, ONW])
        ot_hi = sb("ot_hi", [P, BLK, 6, P], F32R)
        ot_lo = sb("ot_lo", [P, BLK, 6, P], F32R)
        resid = sb("resid", [P, BLK, D])
        y = sb("y", [P, BLK, D])

        ld_keys = [sem(f"ld_keys{kk}") for kk in range(KC)]
        (ld_ident, ld_wkv, ld_wv, ld_wvv, ld_wov, ld_wo, ld_wq, ld_small, vext_zero, vext_const, ktext_ps, ktext_rdy,
         kvip_ps, kvip_raw, kvip_turned, kraw_rdy, khi_rdy, klo_rdy, marks_rdy, kpacked, kdiag0_rdy, kdiag1_rdy,
         kraw_zero, v_ps, v_rdy, vvip_ps, vvip_raw, vvip_turned, vv_rdy, diag_rdy, vw_ps, vwhi_rdy, vwlo_rdy, wqhi_rdy,
         wqlo_rdy, wohi_rdy, wolo_rdy, wqlo_last) = (
            sem(n) for n in ("ld_ident", "ld_wkv", "ld_wv", "ld_wvv", "ld_wov", "ld_wo", "ld_wq", "ld_small",
                             "vext_zero", "vext_const", "ktext_ps", "ktext_rdy", "kvip_ps", "kvip_raw", "kvip_turned",
                             "kraw_rdy", "khi_rdy", "klo_rdy", "marks_rdy", "kpacked", "kdiag0_rdy", "kdiag1_rdy",
                             "kraw_zero", "v_ps", "v_rdy", "vvip_ps", "vvip_raw", "vvip_turned", "vv_rdy",
                             "diag_rdy", "vw_ps", "vwhi_rdy", "vwlo_rdy", "wqhi_rdy", "wqlo_rdy", "wohi_rdy",
                             "wolo_rdy", "wqlo_last"))
        x_in = [sem(f"x_in{b}") for b in range(BATCHES)]
        packed = [sem(f"packed{b}") for b in range(BATCHES)]
        last_packed = [sem(f"last_packed{b}") for b in range(BATCHES)]
        max_in = [sem(f"max_in{b}") for b in range(BATCHES)]
        (xhi_rdy, xlo_main, xlo_rdy, q_ps, qhi_rdy, qlo_rdy, guide_ps, guide_max, nmt_ps, nmhi_rdy, nmlo_rdy, s_ps, p_rdy,
         pv_ps, sums_rdy, on_rdy, ot_ps, othi_rdy, otlo_rdy, y_ps, y_rdy, res_in, y_out) = (
            sem(n) for n in ("xhi_rdy", "xlo_main", "xlo_rdy", "q_ps", "qhi_rdy", "qlo_rdy", "guide_ps", "guide_max", "nmt_ps",
                             "nmhi_rdy", "nmlo_rdy", "s_ps", "p_rdy", "pv_ps", "sums_rdy", "on_rdy", "ot_ps",
                             "othi_rdy", "otlo_rdy", "y_ps", "y_rdy", "res_in", "y_out"))

        def ps(name, shape):
            return ctx.enter_context(nc.psum_tensor(name, shape, F32))

        s_bank = [ps(f"s_bank{i}", [P, 2, TOK]) for i in range(2)]
        v_bank = [ps(f"v_bank{t}", [P, PAIRS, VCOLS]) for t in range(BLK)]
        q_bank = [ps(f"q_bank{i}", [P, 512]) for i in range(2)]
        o_bank = [ps(f"o_bank{i}", [P, 512]) for i in range(2)]
        v_flat = [bank[:].rearrange("p h n -> p (h n)") for bank in v_bank]
        s_flat = [bank[:].rearrange("p a n -> p (a n)") for bank in s_bank]
        key_bank = [q_bank[0], q_bank[1], o_bank[0], o_bank[1], v_flat[0]]
        kvip_bank = [v_flat[1], s_flat[0]]
        value_bank = [o_bank[0][:], o_bank[1][:], s_flat[0], s_flat[1]]
        turn_bank = {(t, False): [o_bank[0], o_bank[1]] for t in range(BLK)}
        turn_bank |= {(0, True): [q_bank[0], q_bank[1]], (1, True): [s_flat[0], s_flat[1]]}
        out_bank = {(t, False): [o_bank[0], o_bank[1]] for t in range(BLK)}
        out_bank |= {(0, True): [o_bank[0], o_bank[1]], (1, True): [v_flat[0], v_flat[1]]}
        block = ctx.enter_context(nc.Block())

        def size(kk):
            return P if kk < FULL else REST

        SMALLS = 4
        KPACKS = 3 * (PARTS + 1) + 1
        PACKS = 3 * PARTS
        MAXES = 2
        JOBS = CHUNKS * BLK
        x_src = dram["xt"]
        r_src = dram["x"].rearrange("b (j t p) e -> b j p t e", t=BLK, p=P)
        y_dst = out.rearrange("b (j t p) e -> b j p t e", t=BLK, p=P)

        def reach(eng, s, count):
            if not (isinstance(count, int) and count <= 0):
                eng.wait_ge(s, count)

        def steps(eng, step):
            step(0, False)
            with eng.Fori(1, STEPS - 1) as j:
                step(j, False)
            step(STEPS - 1, True)

        def next_unit(j, b):
            return (j, 1) if b == 0 else (j + 1, 0)

        def last_unit(j, b):
            return (j, 0) if b == 1 else (j - 1, 1)

        def has_last(j, b):
            return b == 1 or not (isinstance(j, int) and j == 0)

        END = (STEPS - 1, BATCHES - 1)

        @block.sync
        def _(sp):
            def load_x(j, b):
                src = x_src[BATCHES * j + b] if isinstance(j, int) else x_src[bass.ds(BATCHES * j + b, 1)].rearrange("o c n -> (o c) n")
                sp.dma_start(x_raw[:, b, 0:FULL, :], src[0:FULL * P].rearrange("(c p) n -> p c n", p=P)).then_inc(x_in[b], 16)
                for half in range(2):
                    sp.dma_start(x_raw[half * REST:(half + 1) * REST, b, FULL, :], src[FULL * P:D]).then_inc(x_in[b], 16)

            def pack(j, b):
                u = BATCHES * j + b
                sp.wait_ge(qhi_rdy, CHUNKS * u + SHARED)
                sp.wait_ge(qlo_rdy, CHUNKS * u + SHARED)
                for row, src in ((0, q_hi), (2 * HD, q_hi), (HD, q_lo)):
                    sp.dma_start(words(q_pack[row:row + HD, b, HEADS - 1, :]),
                                 words(src[PARTS * HD:PARTS * HD + LASTR, 0:SHARED, :])).then_inc(last_packed[b], 16)
                sp.wait_ge(qhi_rdy, CHUNKS * (u + 1))
                sp.wait_ge(qlo_rdy, CHUNKS * (u + 1))
                for row, src in ((0, q_hi), (2 * HD, q_hi), (HD, q_lo)):
                    for a in range(PARTS):
                        sp.dma_start(words(q_pack[row:row + HD, b, a:a + PARTS * (CHUNKS - 1) + 1:PARTS, :]),
                                     words(src[a * HD:(a + 1) * HD, :, :])).then_inc(packed[b], 16)

            def bring_max(j, b):
                u = BATCHES * j + b
                sp.wait_ge(nmhi_rdy, u + 1)
                sp.dma_start(words(q_pack[MAXROW:MAXROW + 2, b, :, :]), words(nm_hi[:])).then_inc(max_in[b], 16)
                sp.wait_ge(nmlo_rdy, u + 1)
                sp.dma_start(words(q_pack[MAXROW + 2:MAXROW + 4, b, :, :]), words(nm_lo[:])).then_inc(max_in[b], 16)

            def load_residual(j, b):
                if isinstance(j, int) and j == 0 and b == 0:
                    sp.wait_ge(vw_ps, 4)
                reach(sp, y_rdy, 4 * (BATCHES * j + b))
                src = r_src[b, j] if isinstance(j, int) else r_src[b, bass.ds(j, 1)].rearrange("o p t e -> (o p) t e")
                sp.dma_start(resid[:], src).then_inc(res_in, 16)

            def store(j, b):
                sp.wait_ge(y_rdy, 4 * (BATCHES * j + b + 1))
                dst = y_dst[b, j] if isinstance(j, int) else y_dst[b, bass.ds(j, 1)].rearrange("o p t e -> (o p) t e")
                sp.dma_start(dst, y[:]).then_inc(y_out, 16)

            def unit(j, b, last):
                u = BATCHES * j + b
                if not last:
                    sp.wait_ge(xlo_rdy, u + 1)
                    load_x(j + 1, b)
                if has_last(j, b):
                    load_residual(*last_unit(j, b))
                nj, nb = next_unit(j, b)
                if not (last and b == 1):
                    pack(nj, nb)
                    bring_max(nj, nb)
                if has_last(j, b):
                    store(*last_unit(j, b))

            def load(name, dst, landed, twice=False):
                w = dram[name]
                sp.dma_start(dst[:, 0:FULL, :], w[0:FULL * P, :].rearrange("(c p) n -> p c n", p=P)).then_inc(landed, 16)
                for half in range(1 + twice):
                    sp.dma_start(dst[half * REST:(half + 1) * REST, FULL, :], w[FULL * P:D, :]).then_inc(landed, 16)

            for kk in range(KC):
                rows, at = size(kk), kk * P
                sp.dma_start(ctx_t[0:rows, kk], dram["ctx"][at:at + rows, :]).then_inc(ld_keys[kk], 16)
                sp.dma_start(raw_a[0:rows, kk], dram["wk"][at:at + rows, :]).then_inc(ld_keys[kk], 16)
            load("wkv", raw_b, ld_wkv)
            sp.dma_start(ident[:], dram["ident"]).then_inc(ld_ident, 16)
            load_x(0, 0)
            load("wq", raw_c, ld_wq, twice=True)
            sp.dma_start(mask_part[:], dram["mask_part"]).then_inc(ld_small, 16)
            sp.dma_start(mask_head[:], dram["mask_head"]).then_inc(ld_small, 16)
            sp.dma_start(marks_raw[:], dram["marks"]).then_inc(ld_small, 16)
            sp.dma_start(v_const[:], dram["v_const"]).then_inc(ld_small, 16)
            sp.wait_ge(wqhi_rdy, KC)
            sp.wait_ge(wqlo_rdy, FULL)
            sp.wait_ge(wqlo_last, 1)
            load("wv", raw_c, ld_wv)
            sp.wait_ge(ktext_ps, CHUNKS)
            load("wvv", raw_a, ld_wvv)
            load_x(0, 1)
            sp.wait_ge(khi_rdy, 1)
            sp.wait_ge(klo_rdy, 1)
            for row, src in ((0, k_hi), (HD, k_hi), (2 * HD, k_lo)):
                for a in range(PARTS):
                    sp.dma_start(words(k_pack[row:row + HD, a:a + PARTS * (CHUNKS - 1) + 1:PARTS].rearrange("p h b k -> p h (b k)")),
                                 words(src[a * HD:(a + 1) * HD, :, :])).then_inc(kpacked, 16)
                sp.dma_start(words(k_pack[row:row + HD, HEADS - 1].rearrange("p b k -> p (b k)")),
                             words(src[PARTS * HD:PARTS * HD + LASTR, 0:SHARED, :])).then_inc(kpacked, 16)
            sp.wait_ge(marks_rdy, 1)
            sp.dma_start(words(k_pack[MAXROW:MAXROW + 4].rearrange("p h b k -> p (h b) k")),
                         words(marks[:])[:, None, :].to_broadcast([4, HEADS * BATCHES, KEYS])).then_inc(kpacked, 16)
            pack(0, 0)
            bring_max(0, 0)
            load("wov", raw_b, ld_wov)
            sp.wait_ge(v_ps, 4)
            load("wo", raw_c, ld_wo, twice=True)

            def step(j, last):
                for b in range(BATCHES):
                    unit(j, b, last)
            steps(sp, step)
            load_residual(*END)
            for t in range(BLK):
                for n in range(2):
                    sp.wait_ge(y_rdy, 4 * (BATCHES * STEPS - 1) + 2 * t + n + 1)
                    cols = slice(n * HALF, (n + 1) * HALF)
                    sp.dma_start(y_dst[END[1], END[0], :, t, cols], y[:, t, cols]).then_inc(y_out, 16)
            sp.wait_ge(y_out, 16 * (BATCHES * STEPS + 3))

        @block.tensor
        def _(pe):
            def queries(j, b, c):
                u = BATCHES * j + b
                if c == 0:
                    pe.wait_ge(xlo_rdy, u + 1)
                if c < 2:
                    reach(pe, guide_max, JOBS * u)
                else:
                    pe.wait_ge(qlo_rdy, CHUNKS * u + c - 1)
                m, at, bank = SIZES[c], STARTS[c], q_bank[c % 2]
                terms = []
                for kk in range(FULL):
                    terms += [(wq_hi, x_hi, kk, P), (wq_hi, x_lo, kk, P), (wq_lo, x_hi, kk, P)]
                terms += [(wq_hi, x_hi, FULL, P), (wq_lo, x_hi, FULL, REST)]
                for n, (w, x, kk, k) in enumerate(terms):
                    if isinstance(u, int) and u == 0 and c == 0 and w is wq_hi and x is x_hi:
                        pe.wait_ge(*((wqlo_last, 1) if kk == FULL else (wqlo_rdy, kk + 1)))
                    mm = pe.matmul(bank[0:m, 0:TOK], w[0:k, kk, at:at + m], x[0:k, kk, :],
                                   start=(n == 0), stop=(n == len(terms) - 1))
                mm.then_inc(q_ps, 1)

            def guide(j, b, i):
                u = BATCHES * j + b
                c, t = i // BLK, i % BLK
                if i < 2:
                    pe.wait_ge(qlo_rdy, CHUNKS * u + 4 + i)
                else:
                    pe.wait_ge(guide_max, JOBS * u + i - 1)
                bank = q_bank[(i + 1) % 2]
                mm = pe.matmul(bank[:, 0:PARTS * KEYS], q_hi[0:SIZES[c], c, t * P:(t + 1) * P],
                               k_diag[0:SIZES[c], b, c, :, :], start=True, stop=True)
                if c == CHUNKS - 1:
                    pe.wait_ge(last_packed[b], 16 * 3 * (j + 1))
                    mm = pe.matmul(bank[:, PARTS * KEYS:512], q_pack[0:MAXROW, b, HEADS - 1, t * P:(t + 1) * P],
                                   k_pack[0:MAXROW, HEADS - 1, b, :], start=True, stop=True)
                mm.then_inc(guide_ps, 1)

            def turn_max(j, b):
                u = BATCHES * j + b
                pe.wait_ge(guide_max, JOBS * (u + 1))
                reach(pe, p_rdy, PAIRS * u - 1)
                for t in range(BLK):
                    mm = pe.transpose(s_bank[0][0:2 * HEADS, 0, t * P:(t + 1) * P],
                                      neg_max[:, t].rearrange("p g h -> p (g h)"), ident[:])
                mm.then_inc(nmt_ps, 1)

            def scores(j, b, k):
                u = BATCHES * j + b
                if k == 0:
                    pe.wait_ge(packed[b], 16 * PACKS * (j + 1))
                    pe.wait_ge(max_in[b], 16 * MAXES * (j + 1))
                reach(pe, p_rdy, PAIRS * u + k - 1)
                for a in range(2):
                    mm = pe.matmul(s_bank[k % 2][:, a, :], k_pack[:, 2 * k + a, b, :], q_pack[0:QROWS, b, 2 * k + a, :],
                                   start=True, stop=True)
                mm.then_inc(s_ps, 1)

            def values(j, b, k):
                u = BATCHES * j + b
                pe.wait_ge(p_rdy, PAIRS * u + k + 1)
                if k % (PAIRS // 2) == 0:
                    reach(pe, on_rdy, 2 * BLK * u + BLK * (k // (PAIRS // 2)))
                for t in range(BLK):
                    for a in range(2):
                        h = 2 * k + a
                        mm = pe.matmul(v_bank[t][:, h % PAIRS, :], probs[:, k % RING, a, t * P:(t + 1) * P],
                                       v_ext[:, b, h, :], start=True, stop=True)
                mm.then_inc(pv_ps, 1)

            def turn_o(j, b, t, end=False):
                u = BATCHES * j + b
                pe.wait_ge(on_rdy, 2 * BLK * u + BLK + t + 1)
                for half, chunks in enumerate((range(4), range(4, 6))):
                    if isinstance(u, int) and u == 0 and t == 0:
                        pe.wait_ge(vwlo_rdy, 3 + half)
                    elif not end and t == 0:
                        reach(pe, y_rdy, 4 * u - 1 + half)
                    elif not end:
                        pe.wait_ge(otlo_rdy, 4 * u + 1 + half)
                    bank = turn_bank[t, end][half]
                    for c in chunks:
                        mm = pe.transpose(bank[:, (c % 4) * P:(c % 4 + 1) * P], o_norm[:, t, c * P:(c + 1) * P], ident[:])
                    mm.then_inc(ot_ps, 1)

            def output(j, b, t, n, between=None, end=False):
                u = BATCHES * j + b
                if isinstance(u, int) and u == 0 and t == 0 and n == 0:
                    pe.wait_ge(wolo_rdy, KC)
                    pe.wait_ge(vwlo_rdy, 4)
                if end and n == 0:
                    pe.wait_ge(otlo_rdy, 4 * u + 2 * (t + 1))
                if end and t == 0:
                    pe.wait_ge(y_rdy, 4 * u - 1 + n)
                elif not end and t == 0:
                    pe.wait_ge(otlo_rdy, 4 * u + 3 + n)
                elif not end:
                    pe.wait_ge(y_rdy, 4 * u + 1 + n)
                cols = slice(n * HALF, (n + 1) * HALF)
                terms = []
                for c in range(FULL):
                    terms += [(ot_hi, wo_hi[:, c, cols], c, P), (ot_lo, wo_hi[:, c, cols], c, P), (ot_hi, wo_lo[:, c, cols], c, P)]
                terms += [(ot_hi, wo_hi[:, FULL, cols], FULL, P), (ot_hi, wo_lo[0:REST, FULL, cols], FULL, REST)]
                terms += [(ot_hi, vw_hi[:, b, cols], 5, P), (ot_lo, vw_hi[:, b, cols], 5, P), (ot_hi, vw_lo[:, b, cols], 5, P)]
                for i, (o, w, c, k) in enumerate(terms):
                    mm = pe.matmul(out_bank[t, end][n][:, 0:HALF], o[0:k, t, c, :], w, start=(i == 0), stop=(i == len(terms) - 1))
                    if between is not None and i == len(terms) // 2:
                        between()
                mm.then_inc(y_ps, 1)

            def unit(j, b, last):
                nj, nb = next_unit(j, b)
                more, before = not (last and b == 1), has_last(j, b)

                def last_output(g, between=None):
                    if before:
                        output(*last_unit(j, b), g // 2, g % 2, between)
                    else:
                        vip_weights(g // 2, g % 2, between)

                def last_turn(t):
                    if before:
                        turn_o(*last_unit(j, b), t)

                if not more:
                    scores(j, b, 0)
                    last_turn(0)
                    scores(j, b, 1)
                    values(j, b, 0)
                    last_turn(1)
                    values(j, b, 1)
                    scores(j, b, 2)
                    scores(j, b, 3)
                    last_output(0)
                    values(j, b, 2)
                    scores(j, b, 4)
                    values(j, b, 3)
                    scores(j, b, 5)
                    last_output(1)
                    for k in range(4, 6):
                        values(j, b, k)
                        scores(j, b, k + 2)
                    for k in range(6, 8):
                        values(j, b, k)
                    for t in range(BLK):
                        last_output(2 + t)
                        turn_o(j, b, t, end=True)
                    for t in range(BLK):
                        for n in range(2):
                            output(j, b, t, n, end=True)
                    return

                queries(nj, nb, 0)
                if not before:
                    pe.wait_ge(vvip_raw, 2)
                    turn_vip(v_flat[0], [(e * P, size(e)) for e in range(KC)], vvip_turned)
                last_turn(0)
                scores(j, b, 0)
                scores(j, b, 1)
                queries(nj, nb, 1)
                if not before:
                    pe.wait_ge(v_rdy, 4)
                    pe.wait_ge(vext_const, 1)
                    pe.wait_ge(vv_rdy, 2)
                values(j, b, 0)
                last_turn(1)
                values(j, b, 1)
                for k in (2, 3):
                    scores(j, b, k)
                    queries(nj, nb, k)
                    values(j, b, k)
                scores(j, b, 4)
                queries(nj, nb, 4)
                scores(j, b, 5)
                if not before:
                    pe.wait_ge(kdiag1_rdy, PARTS)
                guide(nj, nb, 0)
                last_output(0, between=lambda: guide(nj, nb, 1))
                guide(nj, nb, 2)
                values(j, b, 4)
                guide(nj, nb, 3)
                scores(j, b, 6)
                guide(nj, nb, 4)
                values(j, b, 5)
                guide(nj, nb, 5)
                last_output(1, between=lambda: guide(nj, nb, 6))
                guide(nj, nb, 7)
                guide(nj, nb, 8)
                scores(j, b, 7)
                values(j, b, 6)
                guide(nj, nb, 9)
                values(j, b, 7)
                turn_max(nj, nb)
                last_output(2)
                last_output(3)

            def text_keys(c, kk):
                m, at = SIZES[c], STARTS[c]
                mm = pe.matmul(key_bank[c][0:m, 0:BATCHES * ENC], raw_a[0:size(kk), kk, at:at + m],
                               ctx_t[0:size(kk), kk, 0:BATCHES * ENC], start=(kk == 0), stop=(kk == KC - 1))
                if kk == KC - 1:
                    mm.then_inc(ktext_ps, 1)

            def vip_rows(bank, w, n, made, between=None):
                for kk in range(KC):
                    if between is not None and kk == KC // 2 + 1:
                        between()
                    mm = pe.matmul(bank[0:BATCHES * VIP, 0:HALF], ctx_t[0:size(kk), kk, BATCHES * ENC:],
                                   w[0:size(kk), kk, n * HALF:(n + 1) * HALF], start=(kk == 0), stop=(kk == KC - 1))
                mm.then_inc(made, 1)

            def turn_vip(bank, chunks, turned):
                n = BATCHES * VIP
                for i, (at, m) in enumerate(chunks):
                    mm = pe.transpose(bank[0:m, i * n:(i + 1) * n], vip_raw[:, at:at + m], ident[0:n, 0:n])
                mm.then_inc(turned, 1)

            def text_values(b, n):
                for kk in range(KC):
                    mm = pe.matmul(value_bank[2 * b + n][0:ENC, 0:HALF], ctx_t[0:size(kk), kk, b * ENC:(b + 1) * ENC],
                                   raw_c[0:size(kk), kk, n * HALF:(n + 1) * HALF], start=(kk == 0), stop=(kk == KC - 1))
                mm.then_inc(v_ps, 1)

            def vip_weights(g, n, between=None):
                if g == 0 and n == 0:
                    pe.wait_ge(diag_rdy, len(VW_PARTS[0] + VW_PARTS[1]) * BATCHES)
                    pe.wait_ge(ld_wov, 32)
                    pe.wait_ge(v_rdy, 2)
                if g == 1:
                    pe.wait_ge(vwlo_rdy, n + 1)
                for i, e in enumerate(VW_PARTS[g]):
                    if between is not None and i == 1:
                        between()
                    mm = pe.matmul(o_bank[n][:, 0:HALF], vv_diag[0:size(e), VW_AT[g] + i].rearrange("p b h k -> p (b h k)"),
                                   raw_b[0:size(e), e, n * HALF:(n + 1) * HALF], start=(i == 0), stop=(e == VW_PARTS[g][-1]))
                mm.then_inc(vw_ps, 1)

            for kk in range(KC):
                pe.wait_ge(ld_keys[kk], 32)
                for c in range(CHUNKS):
                    text_keys(c, kk)
            pe.wait_ge(ld_wkv, 32)
            for n in range(2):
                vip_rows(kvip_bank[n], raw_b, n, kvip_ps)
            pe.wait_ge(ktext_rdy, CHUNKS)
            queries(0, 0, 0)
            pe.wait_ge(ld_ident, 16)
            pe.wait_ge(kvip_raw, 2)
            turn_vip(s_flat[1], list(zip(STARTS, SIZES)), kvip_turned)
            for c in range(1, CHUNKS):
                queries(0, 0, c)
            pe.wait_ge(ld_wv, 32)
            pe.wait_ge(kraw_rdy, 1)
            for i in range(4):
                text_values(i // 2, i % 2)
                if i == 0:
                    pe.wait_ge(kdiag0_rdy, PARTS)
                guide(0, 0, 2 * i)
                guide(0, 0, 2 * i + 1)
            pe.wait_ge(ld_wvv, 32)
            vip_rows(v_flat[0], raw_a, 0, vvip_ps)
            pe.wait_ge(kpacked, 16 * KPACKS)
            guide(0, 0, 8)
            guide(0, 0, 9)
            pe.wait_ge(v_rdy, 3)
            vip_rows(v_flat[1], raw_a, 1, vvip_ps, between=lambda: turn_max(0, 0))

            def step(j, last):
                for b in range(BATCHES):
                    unit(j, b, last)
            steps(pe, step)

        @block.gpsimd
        def _(pool):
            def split_x(j, b):
                u = BATCHES * j + b
                pool.wait_ge(xhi_rdy, u + 1)
                nc.gpsimd.tensor_tensor(x_lo[:], x_raw[:, b, 0:FULL], x_hi[:, 0:FULL], ALU.subtract).then_inc(xlo_main, 1)
                pool.wait_ge(xlo_main, u + 1)
                nc.gpsimd.tensor_tensor(x_hi[REST:P, FULL], x_raw[REST:P, b, FULL], x_hi[REST:P, FULL],
                                        ALU.subtract).then_inc(xlo_rdy, 1)
                pool.wait_ge(xlo_rdy, u + 1)

            nc.gpsimd.memset(v_ext[:], 0.0).then_inc(vext_zero, 1)
            split_x(0, 0)
            pool.wait_ge(wqhi_rdy, KC)
            nc.gpsimd.tensor_tensor(wq_lo[:, FULL], raw_c[:, FULL], wq_hi[:, FULL], ALU.subtract).then_inc(wqlo_last, 1)
            pool.wait_ge(ld_small, 16 * SMALLS)
            pool.wait_ge(vext_zero, 1)
            nc.gpsimd.tensor_copy(v_ext[:, :, :, HD:VCOLS].rearrange("p b h n -> p (b h) n"),
                                  v_const[:, None, :].to_broadcast([KEYS, BATCHES * HEADS, VCOLS - HD])).then_inc(vext_const, 1)
            pool.wait_ge(kraw_rdy, 1)
            for a in range(PARTS):
                nc.gpsimd.tensor_scalar(k_diag[:, 1, :, a, :], k_raw[:, :, 1, :], mask_part[0:WIDE, a:a + 1],
                                        None, ALU.mult).then_inc(kdiag1_rdy, 1)
            split_x(0, 1)
            pool.wait_ge(vv_rdy, 2)
            for g in range(2):
                for i, e in enumerate(VW_PARTS[g]):
                    for place in range(BATCHES):
                        m = size(e)
                        nc.gpsimd.tensor_tensor(vv_diag[0:m, VW_AT[g] + i, place],
                                                vv_t[0:m, e, place ^ g, None, :].to_broadcast([m, PAIRS, VIP]),
                                                mask_head[0:m, e, g * PAIRS:(g + 1) * PAIRS, None].to_broadcast([m, PAIRS, VIP]),
                                                ALU.mult).then_inc(diag_rdy, 1)
            split_x(1, 0)
            for c in range(KC):
                pool.wait_ge(wohi_rdy, c + 1)
                nc.gpsimd.tensor_tensor(wo_lo[:, c], raw_c[:, c], wo_hi[:, c], ALU.subtract).then_inc(wolo_rdy, 1)

            def step(j, last):
                for b in range(BATCHES):
                    if not last and not (isinstance(j, int) and j == 0 and b == 0):
                        split_x(j + 1, b)
            steps(pool, step)

        @block.scalar
        def _(act):
            def split_x(j, b):
                u = BATCHES * j + b
                act.wait_ge(x_in[b], 48 * (j + 1))
                reach(act, q_ps, CHUNKS * u)
                nc.scalar.copy(x_hi[:], x_raw[:, b]).then_inc(xhi_rdy, 1)

            def queries(j, b, c):
                u = BATCHES * j + b
                act.wait_ge(q_ps, CHUNKS * u + c + 1)
                if c == 0:
                    reach(act, guide_ps, JOBS * u)
                    reach(act, packed[1 - b], 16 * PACKS * (j + b))
                nc.scalar.copy(q_hi[0:SIZES[c], c, :], q_bank[c % 2][0:SIZES[c], 0:TOK]).then_inc(qhi_rdy, 1)

            def split_max(j, b):
                u = BATCHES * j + b
                act.wait_ge(nmt_ps, u + 1)
                reach(act, max_in[1 - b], 16 * MAXES * (j + b))
                nc.scalar.copy(nm_hi[:], s_bank[0][0:2 * HEADS, 0, :]).then_inc(nmhi_rdy, 1)

            def exponentials(j, b, k):
                u = BATCHES * j + b
                act.wait_ge(s_ps, PAIRS * u + k + 1)
                reach(act, pv_ps, PAIRS * u + k + 1 - RING)
                nc.scalar.activation(probs[:, k % RING], s_bank[k % 2][:], ACT.Exp, scale=SCALE).then_inc(p_rdy, 1)

            def turned(j, b, t, half, end=False):
                u = BATCHES * j + b
                act.wait_ge(ot_ps, 4 * u + 2 * t + half + 1)
                reach(act, y_ps, 4 * u - 2 + 2 * t)
                a, z = (0, 4) if half == 0 else (4, 6)
                bank = turn_bank[t, end][half][:, 0:(z - a) * P]
                nc.scalar.copy(ot_hi[:, t, a:z], bank.rearrange("p (c n) -> p c n", n=P)).then_inc(othi_rdy, 1)

            def split_wo(c):
                act.wait_ge(ld_wo, 48)
                nc.scalar.copy(wo_hi[:, c], raw_c[:, c]).then_inc(wohi_rdy, 1)

            def vip_weights(g, n):
                act.wait_ge(vw_ps, 2 * g + n + 1)
                for place in range(BATCHES):
                    rows, cols = slice(place * VROWS, (place + 1) * VROWS), slice(n * HALF, (n + 1) * HALF)
                    copy = nc.scalar.copy(vw_hi[rows, place ^ g, cols], o_bank[n][rows, 0:HALF])
                copy.then_inc(vwhi_rdy, 1)

            def unit(j, b, last):
                nj, nb = next_unit(j, b)
                more = not (last and b == 1)
                before = has_last(j, b)

                def next_queries(c):
                    if more:
                        queries(nj, nb, c)

                def last_turned(t):
                    if before:
                        turned(*last_unit(j, b), t, 0)
                        turned(*last_unit(j, b), t, 1)

                next_queries(0)
                if more:
                    last_turned(0)
                exponentials(j, b, 0)
                if not more:
                    last_turned(0)
                exponentials(j, b, 1)
                next_queries(1)
                last_turned(1)
                for k in (2, 3, 4):
                    exponentials(j, b, k)
                    next_queries(k)
                    if not before and k > 2:
                        split_wo(k - 3)
                exponentials(j, b, 5)
                if not last:
                    split_x(j + 1, b)
                if not before:
                    vip_weights(0, 0)
                    split_wo(2)
                exponentials(j, b, 6)
                if not before:
                    vip_weights(0, 1)
                    split_wo(3)
                exponentials(j, b, 7)
                if more:
                    split_max(nj, nb)
                if not before:
                    vip_weights(1, 0)
                    split_wo(4)
                    vip_weights(1, 1)

            split_x(0, 0)
            act.wait_ge(ld_wq, 48)
            for kk in range(KC):
                nc.scalar.copy(wq_hi[:, kk], raw_c[:, kk]).then_inc(wqhi_rdy, 1)
            queries(0, 0, 0)
            act.wait_ge(kraw_rdy, 1)
            nc.scalar.copy(k_hi, k_raw[:].rearrange("p c b k -> p c (b k)")).then_inc(khi_rdy, 1)
            queries(0, 0, 1)
            act.wait_ge(ld_small, 16 * SMALLS)
            nc.scalar.copy(marks[:], marks_raw[:]).then_inc(marks_rdy, 1)
            for c in range(2, CHUNKS):
                queries(0, 0, c)
            act.wait_ge(vext_zero, 1)
            for b in range(BATCHES):
                for n in range(2):
                    act.wait_ge(v_ps, 2 * b + n + 1)
                    nc.scalar.copy(v_ext[0:ENC, b, n * PAIRS:(n + 1) * PAIRS, 0:HD],
                                   value_bank[2 * b + n][0:ENC, 0:HALF].rearrange("p (h d) -> p h d", d=HD)).then_inc(v_rdy, 1)
                    if b == 0 and n == 1:
                        split_x(0, 1)
            split_max(0, 0)

            def step(j, last):
                for b in range(BATCHES):
                    unit(j, b, last)
            steps(act, step)
            for t in range(BLK):
                turned(*END, t, 0, end=True)
                turned(*END, t, 1, end=True)

        @block.vector
        def _(dve):
            def queries(j, b, c):
                u = BATCHES * j + b
                dve.wait_ge(qhi_rdy, CHUNKS * u + c + 1)
                nc.vector.tensor_tensor(q_lo[0:SIZES[c], c, :], q_bank[c % 2][0:SIZES[c], 0:TOK], q_hi[0:SIZES[c], c, :],
                                        ALU.subtract).then_inc(qlo_rdy, 1)

            def maximum(j, b, i):
                u = BATCHES * j + b
                c, t = i // BLK, i % BLK
                dve.wait_ge(guide_ps, JOBS * u + i + 1)
                if i == 0:
                    reach(dve, nmt_ps, u)
                heads = PARTS + (c == CHUNKS - 1)
                bank = q_bank[(i + 1) % 2][:, 0:heads * KEYS].rearrange("p (h k) -> p h k", k=KEYS)
                h = PARTS * c
                nc.vector.reduce_max(neg_max[:, t, 0, h:h + heads], bank[:, :, 0:ENC], AX.X, negate=True)
                nc.vector.reduce_max(neg_max[:, t, 1, h:h + heads], bank[:, :, ENC:KEYS], AX.X, negate=True).then_inc(guide_max, 1)

            def split_max(j, b):
                u = BATCHES * j + b
                dve.wait_ge(nmhi_rdy, u + 1)
                nc.vector.tensor_tensor(nm_lo[:], s_bank[0][0:2 * HEADS, 0, :], nm_hi[:], ALU.subtract).then_inc(nmlo_rdy, 1)

            def divide(j, b, half, t):
                u = BATCHES * j + b
                n = 2 * BLK * u + BLK * half + t
                h0, hz = half * PAIRS, (half + 1) * PAIRS
                if t == 0:
                    dve.wait_ge(pv_ps, PAIRS * u + (half + 1) * PAIRS // 2)
                if half == 0 and t == 0:
                    reach(dve, ot_ps, 4 * u)
                bank = v_bank[t]
                nc.vector.reciprocal(r_sums[:, t, h0:hz, :], bank[:, :, HD + VIP:HD + VIP + 2]).then_inc(sums_rdy, 1)
                dve.wait_ge(sums_rdy, n + 1)
                enc = r_sums[:, t, h0:hz, 0:1]
                vip = r_sums[:, t, h0:hz, 1:2]
                nc.vector.tensor_tensor(o_norm[:, t, 0:ONB].rearrange("p (h d) -> p h d", d=32)[:, h0:hz], bank[:, :, 0:32],
                                        enc.to_broadcast([P, PAIRS, 32]), ALU.mult)
                for copy in range(2):
                    at = ONB + copy * HEADS * TAIL
                    nc.vector.tensor_tensor(o_norm[:, t, at:at + HEADS * TAIL].rearrange("p (h d) -> p h d", d=TAIL)[:, h0:hz],
                                            bank[:, :, 32:HD], enc.to_broadcast([P, PAIRS, TAIL]), ALU.mult)
                v0 = (half ^ b) * PAIRS
                nc.vector.tensor_tensor(o_norm[:, t, VIPCOL:ONW].rearrange("p (h k) -> p h k", k=VIP)[:, v0:v0 + PAIRS],
                                        bank[:, :, HD:HD + VIP], vip.to_broadcast([P, PAIRS, VIP]), ALU.mult).then_inc(on_rdy, 1)

            def turned(j, b, t, half, end=False):
                u = BATCHES * j + b
                dve.wait_ge(othi_rdy, 4 * u + 2 * t + half + 1)
                bank = turn_bank[t, end][half]
                if half == 0:
                    nc.vector.tensor_tensor(ot_lo[:, t, 0:4], bank[:, 0:4 * P].rearrange("p (c n) -> p c n", n=P),
                                            ot_hi[:, t, 0:4], ALU.subtract).then_inc(otlo_rdy, 1)
                else:
                    nc.vector.tensor_tensor(ot_lo[:, t, 5], bank[:, P:2 * P], ot_hi[:, t, 5], ALU.subtract)
                    nc.vector.tensor_tensor(ot_hi[REST:P, t, 4], bank[REST:P, 0:P], ot_hi[REST:P, t, 4],
                                            ALU.subtract).then_inc(otlo_rdy, 1)

            def output(j, b, t, n, end=False):
                u = BATCHES * j + b
                dve.wait_ge(y_ps, 4 * u + 2 * t + n + 1)
                if t == 0 and n == 0:
                    dve.wait_ge(res_in, 16 * (u + 1))
                    reach(dve, y_out, 16 * u)
                cols = slice(n * HALF, (n + 1) * HALF)
                nc.vector.tensor_tensor(y[:, t, cols], out_bank[t, end][n][:, 0:HALF], resid[:, t, cols], ALU.add).then_inc(y_rdy, 1)

            def unit(j, b, last):
                nj, nb = next_unit(j, b)
                more = not (last and b == 1)
                before = has_last(j, b)

                def last_output(g):
                    if before:
                        output(*last_unit(j, b), g // 2, g % 2)
                    else:
                        vip_weights(g // 2, g % 2)

                if not more:
                    for t in range(BLK):
                        turned(*last_unit(j, b), t, 0)
                        turned(*last_unit(j, b), t, 1)
                    last_output(0)
                    for t in range(BLK):
                        divide(j, b, 0, t)
                    last_output(1)
                    for t in range(BLK):
                        divide(j, b, 1, t)
                    for t in range(BLK):
                        last_output(2 + t)
                        turned(j, b, t, 0, end=True)
                        turned(j, b, t, 1, end=True)
                    for t in range(BLK):
                        for n in range(2):
                            output(j, b, t, n, end=True)
                    return

                for k in range(CHUNKS):
                    queries(nj, nb, k)
                    if before and k < BLK:
                        turned(*last_unit(j, b), k, 0)
                        turned(*last_unit(j, b), k, 1)
                    if k == 3:
                        for t in range(BLK):
                            divide(j, b, 0, t)
                for i in range(3):
                    maximum(nj, nb, i)
                last_output(0)
                for i in range(3, JOBS):
                    maximum(nj, nb, i)
                last_output(1)
                divide(j, b, 1, 0)
                split_max(nj, nb)
                divide(j, b, 1, 1)
                last_output(2)
                last_output(3)

            def text_keys(c):
                dve.wait_ge(ktext_ps, c + 1)
                nc.vector.tensor_copy(k_raw[0:SIZES[c], c, :, 0:ENC],
                                      key_bank[c][0:SIZES[c], 0:BATCHES * ENC].rearrange("p (b k) -> p b k", b=BATCHES)).then_inc(ktext_rdy, 1)

            def vip_rows(bank, n, made, copied):
                dve.wait_ge(made, n + 1)
                nc.vector.tensor_copy(vip_raw[:, n * HALF:(n + 1) * HALF], bank[0:BATCHES * VIP, 0:HALF]).then_inc(copied, 1)

            def vip_keys():
                dve.wait_ge(kvip_turned, 1)
                n = BATCHES * VIP
                for c0, c1 in ((0, CHUNKS - 1), (CHUNKS - 1, CHUNKS)):
                    m = SIZES[c0]
                    copy = nc.vector.tensor_copy(k_raw[0:m, c0:c1, :, ENC:KEYS],
                                                 s_flat[1][0:m, c0 * n:c1 * n].rearrange("p (c b k) -> p c b k", b=BATCHES, k=VIP))
                copy.then_inc(kraw_rdy, 1)

            def split_wq(kk):
                dve.wait_ge(wqhi_rdy, kk + 1)
                nc.vector.tensor_tensor(wq_lo[:, kk], raw_c[:, kk], wq_hi[:, kk], ALU.subtract).then_inc(wqlo_rdy, 1)

            def vip_weights(g, n):
                dve.wait_ge(vwhi_rdy, 2 * g + n + 1)
                for place in range(BATCHES):
                    rows, cols = slice(place * VROWS, (place + 1) * VROWS), slice(n * HALF, (n + 1) * HALF)
                    part = nc.vector.tensor_tensor(vw_lo[rows, place ^ g, cols], o_bank[n][rows, 0:HALF],
                                                   vw_hi[rows, place ^ g, cols], ALU.subtract)
                part.then_inc(vwlo_rdy, 1)

            nc.vector.memset(k_raw[:, CHUNKS - 1], 0.0).then_inc(kraw_zero, 1)
            dve.wait_ge(kraw_zero, 1)
            for c in range(CHUNKS):
                text_keys(c)
            vip_rows(kvip_bank[0], 0, kvip_ps, kvip_raw)
            for kk in range(FULL):
                split_wq(kk)
            vip_rows(kvip_bank[1], 1, kvip_ps, kvip_raw)
            vip_keys()
            for c in range(CHUNKS):
                queries(0, 0, c)
                if c == 1:
                    dve.wait_ge(khi_rdy, 1)
                    nc.vector.tensor_tensor(k_lo, k_raw[:].rearrange("p c b k -> p c (b k)"), k_hi, ALU.subtract).then_inc(klo_rdy, 1)
                    dve.wait_ge(ld_small, 16 * SMALLS)
                if c >= CHUNKS - PARTS:
                    a = c - (CHUNKS - PARTS)
                    nc.vector.tensor_scalar(k_diag[:, 0, :, a, :], k_raw[:, :, 0, :], mask_part[0:WIDE, a:a + 1],
                                            None, ALU.mult).then_inc(kdiag0_rdy, 1)
            for i in range(JOBS):
                maximum(0, 0, i)
            vip_rows(v_flat[0], 0, vvip_ps, vvip_raw)
            split_max(0, 0)
            vip_rows(v_flat[1], 1, vvip_ps, vvip_raw)
            dve.wait_ge(vvip_turned, 1)
            n = FULL * BATCHES * VIP
            nc.vector.tensor_copy(vv_t[:, 0:FULL], v_flat[0][:, 0:n].rearrange("p (c b k) -> p c b k", c=FULL, b=BATCHES)).then_inc(vv_rdy, 1)
            nc.vector.tensor_copy(vv_t[0:REST, FULL], v_flat[0][0:REST, n:n + BATCHES * VIP].rearrange("p (b k) -> p b k", b=BATCHES)).then_inc(vv_rdy, 1)

            def step(j, last):
                for b in range(BATCHES):
                    unit(j, b, last)
            steps(dve, step)


def kernel(x, ctx_1152, L0_xattn_Wq, L0_xattn_Wk, L0_xattn_Wv, L0_xattn_Wo, L0_xattn_Wk_vip, L0_xattn_Wv_vip,
           L0_xattn_Wo_vip):
    import concourse.bacc as bacc
    from concourse.bass_utils import run_bass_kernel_spmd

    x, ctx = np.asarray(x), np.asarray(ctx_1152)
    B, S, D = x.shape
    keys = ctx.shape[1]
    hd = D // HEADS
    order, _ = channel_order(hd)
    enc = (keys - NUM_VIP) % keys
    vip = keys - enc
    c = np.ascontiguousarray

    def turned(w, rows=slice(None), cols=slice(None)):
        return c(np.asarray(w).T[rows][:, cols])

    mask_part = np.zeros((P, PARTS), np.float32)
    for a in range(PARTS):
        mask_part[a * hd:(a + 1) * hd, a] = 1
    mask_head = np.zeros((P, D // P + 1, HEADS), np.float32)
    for e in range(D):
        mask_head[e % P, e // P, e // hd] = 1
    marks = np.zeros((4, keys), np.float32)
    marks[0::2, :enc] = 1
    marks[1::2, enc:] = 1
    v_const = np.zeros((keys, VCOLS - hd), np.float32)
    for k in range(vip):
        v_const[enc + k, k] = 1
    v_const[:enc, vip] = 1
    v_const[enc:, vip + 1] = 1
    arrays = {
        "x": c(x),
        "xt": c(x.reshape(B, S // TOK, TOK, D).transpose(1, 0, 3, 2).reshape(B * S // TOK, D, TOK)),
        "ctx": c(np.concatenate([ctx[:, :enc].reshape(B * enc, D), ctx[:, enc:].reshape(B * vip, D)]).T),
        "wq": turned(L0_xattn_Wq, cols=order),
        "wk": turned(L0_xattn_Wk, cols=order),
        "wkv": turned(L0_xattn_Wk_vip, cols=order),
        "wv": turned(L0_xattn_Wv),
        "wvv": turned(L0_xattn_Wv_vip),
        "wo": turned(L0_xattn_Wo, rows=output_order(hd)),
        "wov": turned(L0_xattn_Wo_vip),
        "mask_part": mask_part, "mask_head": mask_head, "marks": marks, "v_const": v_const,
        "ident": np.eye(P, dtype=np.float32),
    }
    nc = bacc.Bacc("TRN2", target_bir_lowering=False, num_devices=1)
    dram = {n: nc.dram_tensor(f"in_{n}", a.shape, F32, kind="ExternalInput").ap() for n, a in arrays.items()}
    out = nc.dram_tensor("out", (B, S, D), F32, kind="ExternalOutput").ap()
    build(nc, dram, out)
    r = run_bass_kernel_spmd(nc, [{f"in_{n}": a for n, a in arrays.items()}], core_ids=[0])
    return r.results[0]["out"]
```
